# Optimizing a Trainium2 kernel written in Bass

```python
import numpy as np
import jax
import jax.numpy as jnp

def _softmax(x, axis=-1):
    return jax.nn.softmax(x, axis=axis)
def _gelu(x):
    return jax.nn.gelu(x, approximate=True)
def _silu(x):
    return jax.nn.silu(x)
def _sigmoid(x):
    return jax.nn.sigmoid(x)
def _layernorm(x, axis=-1, eps=1e-5):
    m = jnp.mean(x, axis=axis, keepdims=True)
    v = jnp.var(x, axis=axis, keepdims=True)
    return (x - m) / jnp.sqrt(v + eps)
def _scatter_add(tgt, idx, src, axis=0):
    return tgt.at[idx].add(src)
def _segment_sum(src, seg, n):
    return jax.ops.segment_sum(src, seg, n)

kernel_name = 'mk_adj_preln_d2_adj_512_22462e'

def setup_inputs(seed: int = 0):
    np.random.seed(seed)
    _w = jnp.asarray
    def _rec_inputs():
        import jax
        import jax.numpy as jnp
        _gk = jax.random.key(seed)
        x = -0.0002928 + 1 * jax.random.normal(jax.random.fold_in(_gk, 1), (128, 128, 512), jnp.float32)
        _a = jax.random.bernoulli(jax.random.fold_in(_gk, 2), 0.03125, (128, 128, 128))
        _a = jnp.logical_or(_a, jnp.swapaxes(_a, -1, -2))
        _a = jnp.logical_or(_a, jnp.eye(128, dtype=bool))
        adj = _a
        return x, adj
    x, adj = _rec_inputs()
    def _L0_gnn_setup():
        import jax, jax.numpy as jnp
        import numpy as np
        HEAD_NUM = 8
        THRESHOLD = 0.1
        NEG = -10000000000.0
        COS_EPS = 1e-08
        B, S, D = (8, 1024, 512)
        D_OUT = 512
        key = jax.random.key(seed)
        ks = jax.random.split(key, 12)
        embs = jax.random.normal(ks[0], (B, S, D), dtype=jnp.float32)
        lengths = jax.random.randint(ks[1], (B,), S // 2, S + 1)
        pad = jnp.arange(S)[None, :] >= lengths[:, None]
        score_mask = pad[:, :, None] | pad[:, None, :]
        sc = 1.0 / np.sqrt(D)
        mk = lambda k, shp: jax.random.normal(k, shp, dtype=jnp.float32) * sc
        return {'embs': embs, 'score_mask': score_mask, 'map_w': mk(ks[2], (D, D)), 'map_b': jnp.zeros((D,), jnp.float32), 'q_w': mk(ks[3], (D, D)), 'q_b': jnp.zeros((D,), jnp.float32), 'k_w': mk(ks[4], (D, D)), 'k_b': jnp.zeros((D,), jnp.float32), 'gcn_map_w': mk(ks[5], (D_OUT, D)), 'gcn_map_b': jnp.zeros((D_OUT,), jnp.float32), 'gcn_W': jax.random.normal(ks[6], (D_OUT // HEAD_NUM, D_OUT // HEAD_NUM), dtype=jnp.float32) * (1.0 / np.sqrt(D_OUT // HEAD_NUM))}
    _L0_gnn_all = _L0_gnn_setup()
    _L0_gnn_in = {k: v for k, v in _L0_gnn_all.items() if k in ('map_w', 'map_b', 'q_w', 'q_b', 'k_w', 'k_b', 'gcn_map_w', 'gcn_map_b', 'gcn_W', )}
    del _L0_gnn_all

    def _L1_gnn_setup():
        import jax, jax.numpy as jnp
        import numpy as np
        QUERY_DIM = 512
        HEADS = 4
        DIM_HEAD = 64
        INNER = HEADS * DIM_HEAD
        B, N = (4, 2048)
        key = jax.random.key(seed)
        ks = jax.random.split(key, 6)
        s = 1.0 / np.sqrt(QUERY_DIM)
        x = jax.random.normal(ks[0], (B, N, QUERY_DIM), dtype=jnp.float32)
        adjacency_mask = jax.random.randint(ks[1], (B, N, N), 0, 2) > 0
        Wq = jax.random.normal(ks[2], (QUERY_DIM, INNER), dtype=jnp.float32) * s
        Wk = jax.random.normal(ks[3], (QUERY_DIM, INNER), dtype=jnp.float32) * s
        Wv = jax.random.normal(ks[4], (QUERY_DIM, INNER), dtype=jnp.float32) * s
        Wo = jax.random.normal(ks[5], (INNER, QUERY_DIM), dtype=jnp.float32) * (1.0 / np.sqrt(INNER))
        bo = jnp.zeros((QUERY_DIM,), dtype=jnp.float32)
        return {'x': x, 'adjacency_mask': adjacency_mask, 'Wq': Wq, 'Wk': Wk, 'Wv': Wv, 'Wo': Wo, 'bo': bo}
    _L1_gnn_all = _L1_gnn_setup()
    _L1_gnn_in = {k: v for k, v in _L1_gnn_all.items() if k in ('Wq', 'Wk', 'Wv', 'Wo', 'bo', )}
    del _L1_gnn_all

    return {
        "x": x,
        "adj": adj,
        "L0_gnn_map_w": _L0_gnn_in["map_w"],
        "L0_gnn_map_b": _L0_gnn_in["map_b"],
        "L0_gnn_q_w": _L0_gnn_in["q_w"],
        "L0_gnn_q_b": _L0_gnn_in["q_b"],
        "L0_gnn_k_w": _L0_gnn_in["k_w"],
        "L0_gnn_k_b": _L0_gnn_in["k_b"],
        "L0_gnn_gcn_map_w": _L0_gnn_in["gcn_map_w"],
        "L0_gnn_gcn_map_b": _L0_gnn_in["gcn_map_b"],
        "L0_gnn_gcn_W": _L0_gnn_in["gcn_W"],
        "L1_gnn_Wq": _L1_gnn_in["Wq"],
        "L1_gnn_Wk": _L1_gnn_in["Wk"],
        "L1_gnn_Wv": _L1_gnn_in["Wv"],
        "L1_gnn_Wo": _L1_gnn_in["Wo"],
        "L1_gnn_bo": _L1_gnn_in["bo"],
    }

def reference(x, adj, L0_gnn_map_w, L0_gnn_map_b, L0_gnn_q_w, L0_gnn_q_b, L0_gnn_k_w, L0_gnn_k_b, L0_gnn_gcn_map_w, L0_gnn_gcn_map_b, L0_gnn_gcn_W, L1_gnn_Wq, L1_gnn_Wk, L1_gnn_Wv, L1_gnn_Wo, L1_gnn_bo):
    import jax
    import jax.numpy as jnp
    def _L0_gnn_ref(embs, score_mask, map_w, map_b, q_w, q_b, k_w, k_b, gcn_map_w, gcn_map_b, gcn_W):
        import jax, jax.numpy as jnp
        import numpy as np
        HEAD_NUM = 8
        THRESHOLD = 0.1
        NEG = -10000000000.0
        COS_EPS = 1e-08
        B, S, D = (8, 1024, 512)
        D_OUT = 512
        b, s, d = embs.shape
        h, dk = (HEAD_NUM, d // HEAD_NUM)
        sm = score_mask[:, None, :, :]
        keep = (~sm[..., 0:1]).astype(embs.dtype)
        m = embs @ map_w.T + map_b
        sem = m.reshape(b, s, h, dk).transpose(0, 2, 1, 3)
        norm = jnp.maximum(jnp.linalg.norm(sem, axis=-1, keepdims=True), COS_EPS)
        n = sem / norm
        cos = jnp.einsum('bhsd,bhtd->bhst', n, n)
        cos = cos * (~sm).astype(cos.dtype)
        cos_adj = (cos > THRESHOLD).astype(embs.dtype)
        q = (m @ q_w.T + q_b).reshape(b, s, h, dk).transpose(0, 2, 1, 3)
        k = (m @ k_w.T + k_b).reshape(b, s, h, dk).transpose(0, 2, 1, 3)
        scores = jnp.einsum('bhsd,bhtd->bhst', q, k) / jnp.sqrt(jnp.asarray(dk, embs.dtype))
        scores = jnp.where(sm, NEG, scores)
        p_attn = jax.nn.softmax(scores, axis=-1) * keep
        adj = cos_adj * p_attn
        hk = gcn_map_w.shape[0] // h
        sem_h = (embs @ gcn_map_w.T + gcn_map_b).reshape(b, s, h, hk).transpose(2, 0, 1, 3)
        adj_h = adj.transpose(1, 0, 2, 3)
        Ax = jnp.einsum('hbst,hbtd->hbsd', adj_h, sem_h)
        AxW = Ax @ gcn_W.T
        denom = adj_h.sum(-1, keepdims=True) + 1.0
        out = jax.nn.relu(AxW / denom)
        out = out.transpose(1, 2, 0, 3).reshape(b, s, h * hk)
        return out

    def _L1_gnn_ref(x, adjacency_mask, Wq, Wk, Wv, Wo, bo):
        import jax, jax.numpy as jnp
        import numpy as np
        QUERY_DIM = 512
        HEADS = 4
        DIM_HEAD = 64
        INNER = HEADS * DIM_HEAD
        B, N = (4, 2048)
        scale = DIM_HEAD ** (-0.5)

        def split_heads(t):
            b, n, _ = t.shape
            return t.reshape(b, n, HEADS, DIM_HEAD).transpose(0, 2, 1, 3)
        q = split_heads(x @ Wq)
        k = split_heads(x @ Wk)
        v = split_heads(x @ Wv)
        sim = jnp.einsum('bhid,bhjd->bhij', q, k) * scale
        neg = -jnp.finfo(sim.dtype).max
        sim = jnp.where(adjacency_mask[:, None, :, :], sim, neg)
        attn = jax.nn.softmax(sim, axis=-1)
        out = jnp.einsum('bhij,bhjd->bhid', attn, v)
        out = out.transpose(0, 2, 1, 3).reshape(x.shape[0], x.shape[1], INNER)
        return out @ Wo + bo

    h = jnp.maximum(_layernorm(x, axis=-1), 0.0)
    x = x + _L0_gnn_ref(h, adj, L0_gnn_map_w, L0_gnn_map_b, L0_gnn_q_w, L0_gnn_q_b, L0_gnn_k_w, L0_gnn_k_b, L0_gnn_gcn_map_w, L0_gnn_gcn_map_b, L0_gnn_gcn_W)
    h = jnp.maximum(_layernorm(x, axis=-1), 0.0)
    x = x + _L1_gnn_ref(h, adj, L1_gnn_Wq, L1_gnn_Wk, L1_gnn_Wv, L1_gnn_Wo, L1_gnn_bo)
    return x


_drawn_inputs = setup_inputs


def setup_inputs(seed=0):
    import zlib

    import numpy as np

    out = dict(_drawn_inputs(seed))
    spreads = {'L0_gnn_map_b': (0.0, 0.8),
     'L0_gnn_q_b': (0.0, 0.8),
     'L0_gnn_k_b': (0.0, 0.8),
     'L0_gnn_gcn_map_b': (0.0, 0.1),
     'L1_gnn_bo': (0.0, 0.1)}
    factors = {'L0_gnn_map_w': 5.765, 'L0_gnn_q_w': 7.156, 'L0_gnn_k_w': 7.174}
    for name, (base, spread) in spreads.items():
        noise = np.random.default_rng([zlib.crc32(name.encode()), seed]).standard_normal(out[name].shape)
        drawn = base * np.exp(spread * noise) if base else spread * noise
        out[name] = jnp.asarray(drawn.astype(out[name].dtype))
    for name, factor in factors.items():
        out[name] = (out[name] * factor).astype(out[name].dtype)
    return out
```

```python
from contextlib import ExitStack

import concourse.bass as bass
from concourse import mybir

F32 = mybir.dt.float32
F32R = mybir.dt.float32r
BF16 = mybir.dt.bfloat16
U8 = mybir.dt.uint8
ALU = mybir.AluOpType
ACT = mybir.ActivationFunctionType
AX_X = mybir.AxisListType.X

P = 128
UNROLL = 4
BLOCKED = 1e30
LN_EPS = 1e-5
COS_EPS = 1e-8
THRESHOLD = 0.1

PROJ_UNITS = (
    (("m0", 2), ("m1", 2), ("m2", 2), ("m3", 2), ("v1a", -2), ("v1b", -1), ("va", 2), ("vb", 3), ("wo", -4)),
    (("q0", 1), ("q1", 1), ("q2", 1), ("q3", 1), ("k0", 1), ("k1", 1), ("k2", 1), ("k3", 1),
     ("lq0", -3), ("lq1", -3), ("wo", -4), ("lk0", -3), ("lk1", -3)),
)
MIX_UNITS = (
    (("s1", -4), ("p1t", -4), ("pv1", -4)),
    (("s1", -4), ("norm", 1), ("p1t", -4), ("pv1", -4), ("bc0", 1), ("bc1", 2), ("ht0", 3), ("ht1", 4),
     ("h1t0", -1), ("h1t1", 0)),
)
SPLIT_UNITS = ("pv1", "ht0", "ht1", "h1t0", "h1t1")


class Unit:

    def __init__(self, bank, before, full):
        self.bank, self.before, self.full = bank, before, full


class Slot:

    def __init__(self, n, i, graphs):
        self.n, self.i, self.graphs = n, i, graphs
        self.odd = n % 2

    def at(self, f):
        if self.i is None:
            return f(self.n)
        rate = f(self.n + UNROLL) - f(self.n)
        assert f(self.n) > 0 or rate == 0
        return f(self.n) + self.i * rate if rate else f(self.n)

    def has(self, ahead):
        return 0 <= self.n + ahead < self.graphs

    def graph(self, ahead):
        return self.at(lambda t: t + ahead)

    def _unit(self, units, name, back):
        def index(t):
            n = 0
            for u in range(FIRST_SLOT, t):
                n += sum(0 <= u + ahead < self.graphs for _, ahead in units[u % 2])
            for what, ahead in units[t % 2]:
                if what == name:
                    return n
                n += 0 <= t + ahead < self.graphs
            raise KeyError(name)

        at = Slot(self.n - back, self.i, self.graphs)
        return Unit(index(at.n) % 2, at.at(lambda t: index(t) // 2), at.at(lambda t: index(t) + 1))

    def hi_parts(self, name):
        def count(t):
            n = 0
            for u in range(FIRST_SLOT, t + 1):
                for what, ahead in MIX_UNITS[u % 2]:
                    n += what in SPLIT_UNITS and 0 <= u + ahead < self.graphs
                    if u == t and what == name:
                        return n
            raise KeyError(name)
        return self.at(count)

    def proj(self, name, back=0):
        return self._unit(PROJ_UNITS, name, back)

    def mix(self, name, back=0):
        return self._unit(MIX_UNITS, name, back)


FIRST_SLOT = -6
LOOP_FROM = 8
MOST_AHEAD = 6


def wait(engine, sem, count):
    if isinstance(count, int) and count <= 0:
        return
    engine.wait_ge(sem, count)


def settle(engine, sem, loop):
    if loop is not None:
        engine.sem_inc(sem, 1)


def over_slots(engine, graphs, body):
    last = graphs + 4
    loops = (graphs - MOST_AHEAD - LOOP_FROM) // UNROLL
    loop_to = LOOP_FROM + UNROLL * loops
    for n in range(FIRST_SLOT, LOOP_FROM):
        body(Slot(n, None, graphs))
    with engine.Fori(0, loops) as i:
        for j in range(UNROLL):
            body(Slot(LOOP_FROM + j, i, graphs))
    for n in range(loop_to, last):
        body(Slot(n, None, graphs))


def build(nc, x, adj, map_w, map_b, q_w, q_b, k_w, k_b, gcn_map_w, gcn_map_b, gcn_W, Wq, Wk, Wv, Wo, bo, out):
    B, S, D = x.shape
    assert S == P and B % UNROLL == 0
    H = D // gcn_W.shape[0]
    DK = D // H
    C = D // P
    INNER = Wq.shape[1]
    DH = 64
    H1 = INNER // DH
    C1 = INNER // P
    SCALE = float(DK) ** -0.5
    assert DK == 64 and DH == 64 and H == 8 and H1 == 4

    with ExitStack() as ctx:
        def sb(name, shape, dt=F32):
            return ctx.enter_context(nc.sbuf_tensor(name, shape, dt))

        def sem(name):
            return ctx.enter_context(nc.semaphore(name))

        w_m = [sb(f"w_m_{s}", [P, C, D], F32R) for s in ("hi", "lo")]
        w_q = [sb(f"w_q_{s}", [P, C, D], F32R) for s in ("hi", "lo")]
        w_k = [sb(f"w_k_{s}", [P, C, D], F32R) for s in ("hi", "lo")]
        w_v = [sb(f"w_v_{s}", [P, C, D], F32R) for s in ("hi", "lo")]
        w_lq = [sb(f"w_lq_{s}", [P, C, INNER], F32R) for s in ("hi", "lo")]
        w_lk = [sb(f"w_lk_{s}", [P, C, INNER], F32R) for s in ("hi", "lo")]
        w_lv = [sb(f"w_lv_{s}", [P, C, INNER], F32R) for s in ("hi", "lo")]
        w_o = [sb(f"w_o_{s}", [P, C1, D], F32R) for s in ("hi", "lo")]
        ident = sb("ident", [P, P])
        ident_bf = sb("ident_bf", [P, P], BF16)
        head_sel = sb("head_sel", [P, C, H])
        minus_half = sb("minus_half", [P, 2 * H])
        col_map_b = sb("col_map_b", [P, C])
        col_qb = sb("col_qb", [P, C])
        col_kb = sb("col_kb", [P, C])
        col_gb = sb("col_gb", [P, C])
        bias_q = sb("bias_q", [P, C])
        bias_k = sb("bias_k", [P, C])
        bias_v = sb("bias_v", [P, D])
        bias_o = sb("bias_o", [P, D])
        gcn_bd = sb("gcn_bd", [P, P])
        gcn_bd_t = sb("gcn_bd_t", [P, P])
        xa = sb("xa", [P, 2, D])
        xres = sb("xres", [P, D])
        hbuf = sb("hbuf", [P, 4, D])
        x1 = sb("x1", [P, 4, D])
        ybuf = sb("ybuf", [P, 2, D])
        adj_in = sb("adj_in", [P, 4, P], U8)
        block0 = sb("block0", [P, 2, P], BF16)
        block1 = sb("block1", [P, 4, P], BF16)
        keep = sb("keep", [P, 4])
        h_t = [sb(f"h_t_{s}", [P, C, 2 * P], F32R) for s in ("hi", "lo")]
        h1_t = [sb(f"h1_t_{s}", [P, C, 2 * P], F32R) for s in ("hi", "lo")]
        m_sb = sb("m_sb", [P, C, 2 * P])
        dir_t = sb("dir_t", [P, C, 2 * P])
        dir_bd = sb("dir_bd", [P, C, 2, 2, P])
        q_t = sb("q_t", [P, C, 2 * P])
        k_bd = sb("k_bd", [P, C, 2, 2, P])
        v_sb = sb("v_sb", [P, 4, H, DK + 1])
        e_sb = sb("e_sb", [P, H, P])
        ec_t = sb("ec_t", [P, H, P])
        lq_t = sb("lq_t", [P, C1, 2 * P])
        lk_bd = sb("lk_bd", [P, C1, 2, 2, P])
        lv_sb = sb("lv_sb", [P, 4, INNER])
        p1_sb = sb("p1_sb", [P, H1, P])
        p1_t = sb("p1_t", [P, H1, P])
        o_t = [sb(f"o_t_{s}", [P, C1, P], F32R) for s in ("hi", "lo")]
        inv_rows = p1_t[:, :, :].rearrange("p h (a d) -> p (h a) d", d=DK)
        stats0 = sb("stats0", [P, 2, 6])
        mv0 = sb("mv0", [P, 2, 2])
        ve0 = sb("ve0", [P, 2])
        nm0 = sb("nm0", [P, 2])
        rstd0 = sb("rstd0", [P, 2])
        shift0 = sb("shift0", [P, 2])
        stats1 = sb("stats1", [P, 6])
        mv1 = sb("mv1", [P, 2])
        ve1 = sb("ve1", [P, 1])
        nm1 = sb("nm1", [P, 1])
        rstd1 = sb("rstd1", [P, 1])
        shift1 = sb("shift1", [P, 1])
        sq_sum = sb("sq_sum", [P, 2 * H])
        inv_norm = sb("inv_norm", [P, 2 * H])
        mx = sb("mx", [P, H])
        neg_mx = sb("neg_mx", [P, H])
        row_sum = sb("row_sum", [P, 2, H])
        den = sb("den", [P, H])
        inv_den = sb("inv_den", [P, H])
        gain = sb("gain", [P, H])
        lmx = sb("lmx", [P, H1])
        neg_lmx = sb("neg_lmx", [P, H1])
        lsum = sb("lsum", [P, H1])
        inv_lsum = sb("inv_lsum", [P, H1])

        s_ps = ctx.enter_context(nc.psum_tensor("s_ps", [P, 2, 4, P], F32))
        c_ps = ctx.enter_context(nc.psum_tensor("c_ps", [P, 2, 4 * P], F32))
        proj_ps = ctx.enter_context(nc.psum_tensor("proj_ps", [P, 2, 4 * P], F32))
        mix_ps = ctx.enter_context(nc.psum_tensor("mix_ps", [P, 2, 4 * P], F32))

        def av(a):
            return c_ps[:, a, 0:4 * (DK + 1)].rearrange("p (h d) -> p h d", h=4)

        w_in = sem("w_in")
        consts = sem("consts")
        ones_in = sem("ones_in")
        prep_full = sem("prep_full")
        prep_hi = sem("prep_hi")
        prep_copied = sem("prep_copied")
        lw_hi = sem("lw_hi")
        lw_done = sem("lw_done")
        x_in = [sem(f"x_in{i}") for i in range(2)]
        a_in = [sem(f"a_in{i}") for i in range(4)]
        xres_in = sem("xres_in")
        y_out = [sem(f"y_out{i}") for i in range(2)]
        proj_full = sem("proj_full")
        proj_out = [sem(f"proj_out{i}") for i in range(2)]
        mix_full = sem("mix_full")
        mix_out = [sem(f"mix_out{i}") for i in range(2)]
        s_full = sem("s_full")
        c_full = sem("c_full")
        ect_full = sem("ect_full")
        av_full = sem("av_full")
        blocked0 = sem("blocked0")
        blocked1 = sem("blocked1")
        kept = sem("kept")
        stats0_done = sem("stats0_done")
        mv0_done = sem("mv0_done")
        ln0_step = sem("ln0_step")
        h_done = sem("h_done")
        stats1_done = sem("stats1_done")
        mv1_done = sem("mv1_done")
        ln1_step = sem("ln1_step")
        h1_done = sem("h1_done")
        squared = sem("squared")
        inv_norm_done = sem("inv_norm_done")
        inv_rows_done = sem("inv_rows_done")
        mx_done = sem("mx_done")
        neg_mx_done = sem("neg_mx_done")
        e_done = sem("e_done")
        ec_done = sem("ec_done")
        ect_act = sem("ect_act")
        ect_dve = sem("ect_dve")
        den_done = sem("den_done")
        inv_den_done = sem("inv_den_done")
        gain_done = sem("gain_done")
        av_scaled = sem("av_scaled")
        x1_done = sem("x1_done")
        lmx_done = sem("lmx_done")
        neg_lmx_done = sem("neg_lmx_done")
        inv_lsum_done = sem("inv_lsum_done")
        p1_done = sem("p1_done")
        hi_done = sem("hi_done")
        y_base = sem("y_base")
        settled_sp = sem("settled_sp")
        settled_pool = sem("settled_pool")
        settled_dve = sem("settled_dve")

        st_map, st_q, st_k, st_gcn = (
            x1[:, :, :], hbuf[:, :, :],
            dir_bd[:, :, :, :, :].rearrange("p c g a b -> p c (g a b)"),
            k_bd[:, :, :, :, :].rearrange("p c g a b -> p c (g a b)"))
        st_t = v_sb[:, :, :, :].rearrange("p a h d -> p (a h d)")[:, 0:C * D].rearrange("p (c n) -> p c n", c=C)
        st_l = [(m_sb[:, :, :], Wq, w_lq), (dir_t[:, :, :], Wk, w_lk),
                (e_sb[:, :, :].rearrange("p (c a) n -> p c (a n)", c=C), Wv, w_lv),
                (ec_t[:, :, :].rearrange("p (c a) n -> p c (a n)", c=C1), Wo, w_o)]

        def prep_bank(u):
            return (proj_ps, mix_ps)[u % 4 // 2][:, u % 2]

        PREP = ([("split", w_m, c) for c in range(C)]
                + [("turn", st_q, c) for c in range(C)] + [("split", w_q, c) for c in range(C)] + [("bias", bias_q, col_qb)]
                + [("turn", st_k, c) for c in range(C)] + [("split", w_k, c) for c in range(C)] + [("bias", bias_k, col_kb)]
                + [("gcn", None, 0)] + [("split", w_v, c) for c in range(C)] + [("bias_v", None, 0)])
        W_LOADS = 15

        block = ctx.enter_context(nc.Block())

        @block.sync
        def _(sp):
            for dst, src in ((st_map, map_w), (st_q, q_w), (st_k, k_w), (st_gcn, gcn_map_w)):
                sp.dma_start(dst, src.rearrange("(c p) n -> p c n", p=P)).then_inc(w_in, 16)
            for dst, src, _ in st_l:
                sp.dma_start(dst, src.rearrange("(c p) n -> p c n", p=P)).then_inc(w_in, 16)
            for dst, src in ((col_map_b, map_b), (col_qb, q_b), (col_kb, k_b), (col_gb, gcn_map_b)):
                sp.dma_start(dst[:, :], src.rearrange("(c p) -> p c", p=P),
                             allow_slow_non_contiguous=True).then_inc(w_in, 16)
            sp.dma_start(bias_o[:, :], bo.rearrange("(a n) -> a n", a=1).broadcast_to([P, D])).then_inc(w_in, 16)
            sp.wait_ge(consts, 1)
            for a in range(2):
                sp.dma_start(gcn_bd[a * DK:(a + 1) * DK, a * DK:(a + 1) * DK], gcn_W).then_inc(w_in, 16)

            def slot(s):
                if s.has(3):
                    wait(sp, blocked1, s.at(lambda t: t + 3 - 3))
                    settle(sp, settled_sp, s.i)
                    sp.dma_start(adj_in[:, (s.n + 3) % 4, :], adj[s.graph(3)]).then_inc(a_in[(s.n + 3) % 4], 16)
                if s.has(0):
                    wait(sp, x1_done, s.at(lambda t: t))
                    settle(sp, settled_sp, s.i)
                    sp.dma_start(xres[:, :], x[s.graph(0)]).then_inc(xres_in, 16)
                if s.has(6):
                    wait(sp, h_done, s.at(lambda t: t + 6 - 1))
                    settle(sp, settled_sp, s.i)
                    sp.dma_start(xa[:, s.n % 2, :], x[s.graph(6)]).then_inc(x_in[s.n % 2], 16)
                if s.has(-4):
                    u = s.proj("wo")
                    sp.wait_ge(proj_out[u.bank], u.before + 1)
                    settle(sp, settled_sp, s.i)
                    sp.dma_start(out[s.graph(-4)], ybuf[:, s.n % 2, :]).then_inc(y_out[s.n % 2], 16)

            over_slots(sp, B, slot)
            for a in range(2):
                sp.wait_ge(y_out[a], 16 * (B // 2))

        @block.gpsimd
        def _(pool):
            nc.gpsimd.memset(gcn_bd[:, :], 0.0).then_inc(consts, 1)
            nc.gpsimd.memset(ident[:, :], 0.0).then_inc(consts, 1)
            nc.gpsimd.memset(ident_bf[:, :], 0.0).then_inc(consts, 1)
            nc.gpsimd.memset(head_sel[:, :, :], 0.0).then_inc(consts, 1)
            nc.gpsimd.memset(minus_half[:, :], -0.5).then_inc(consts, 1)
            pool.wait_ge(consts, 5)
            for m in (ident, ident_bf):
                nc.gpsimd.affine_select(out=m[:, :], in_=m[:, :], compare_op=ALU.not_equal, fill=1.0, base=0,
                                        pattern=[[-1, P]], channel_multiplier=1).then_inc(consts, 1)
            flat = head_sel[:, :, :].rearrange("p c h -> p (c h)")
            pool.wait_ge(consts, 7)
            for a in range(2):
                nc.gpsimd.memset(flat[a * DK:(a + 1) * DK, a:a + (C - 1) * (H + 2) + 1:H + 2], 1.0).then_inc(consts, 1)

            def slot(s):
                if s.odd and s.has(1):
                    for c in (2, 3):
                        u = s.proj(f"m{c}", back=1)
                        pool.wait_ge(proj_out[u.bank], u.before + 1)
                    wait(pool, c_full, s.at(lambda t: t + 1))
                    nc.gpsimd.tensor_tensor(dir_t[:, :, :], m_sb[:, :, :], m_sb[:, :, :], ALU.mult).then_inc(squared, 1)
                if s.has(1):
                    r = (s.n + 1) % 4
                    pool.wait_ge(a_in[r], s.at(lambda t: 16 * ((t + 1) // 4 + 1)))
                    wait(pool, s_full, s.at(lambda t: t))
                    settle(pool, settled_pool, s.i)
                    nc.gpsimd.tensor_scalar(block0[:, (s.n + 1) % 2, :], adj_in[:, r, :], -BLOCKED, None,
                                            ALU.mult).then_inc(blocked0, 1)
                    wait(pool, x1_done, s.at(lambda t: t - 2))
                    settle(pool, settled_pool, s.i)
                    nc.gpsimd.tensor_scalar(keep[:, r:r + 1], adj_in[:, r, 0:1], -1.0, 1.0, ALU.mult,
                                            ALU.add).then_inc(kept, 1)
                if s.has(0):
                    if s.has(-4):
                        pool.wait_ge(mix_full, s.mix("s1").full)
                    settle(pool, settled_pool, s.i)
                    nc.gpsimd.tensor_scalar(block1[:, s.n % 4, :], adj_in[:, s.n % 4, :], -1.0, BLOCKED, ALU.add,
                                            ALU.mult).then_inc(blocked1, 1)
                if s.has(-4):
                    wait(pool, y_out[s.n % 2], s.at(lambda t: 16 * ((t - 4) // 2)))
                    nc.gpsimd.tensor_tensor(ybuf[:, s.n % 2, :], x1[:, s.n % 4, :], bias_o[:, :],
                                            ALU.add).then_inc(y_base, 1)
                if s.odd and s.has(1):
                    u = s.mix("norm")
                    pool.wait_ge(mix_out[u.bank], u.before + 1)
                    nc.gpsimd.tensor_tensor(inv_norm[:, :], sq_sum[:, :], minus_half[:, :], ALU.pow).then_inc(inv_norm_done, 1)
                if not s.odd and s.has(4):
                    before = s.at(lambda t: 4 * ((t + 4) // 2))
                    pool.wait_ge(mv0_done, s.at(lambda t: t + 4 + 2))
                    wait(pool, h_done, s.at(lambda t: t + 4))
                    settle(pool, settled_pool, s.i)
                    nc.gpsimd.tensor_scalar(ve0[:, :], mv0[:, :, 1], LN_EPS, None, ALU.add).then_inc(ln0_step, 1)
                    nc.gpsimd.tensor_scalar(nm0[:, :], mv0[:, :, 0], -1.0, None, ALU.mult).then_inc(ln0_step, 1)
                    pool.wait_ge(ln0_step, before + 2)
                    nc.gpsimd.tensor_tensor(rstd0[:, :], ve0[:, :], minus_half[:, 0:2], ALU.pow).then_inc(ln0_step, 1)
                    pool.wait_ge(ln0_step, before + 3)
                    nc.gpsimd.tensor_tensor(shift0[:, :], nm0[:, :], rstd0[:, :], ALU.mult).then_inc(ln0_step, 1)
                if s.has(0):
                    before = s.at(lambda t: 4 * t)
                    pool.wait_ge(mv1_done, s.at(lambda t: t + 1))
                    wait(pool, h1_done, s.at(lambda t: t))
                    settle(pool, settled_pool, s.i)
                    nc.gpsimd.tensor_scalar(ve1[:, :], mv1[:, 1:2], LN_EPS, None, ALU.add).then_inc(ln1_step, 1)
                    nc.gpsimd.tensor_scalar(nm1[:, :], mv1[:, 0:1], -1.0, None, ALU.mult).then_inc(ln1_step, 1)
                    pool.wait_ge(ln1_step, before + 2)
                    nc.gpsimd.tensor_tensor(rstd1[:, :], ve1[:, :], minus_half[:, 0:1], ALU.pow).then_inc(ln1_step, 1)
                    pool.wait_ge(ln1_step, before + 3)
                    nc.gpsimd.tensor_tensor(shift1[:, :], nm1[:, :], rstd1[:, :], ALU.mult).then_inc(ln1_step, 1)

                if s.odd and s.has(1):
                    pool.wait_ge(inv_norm_done, s.at(lambda t: (t + 1) // 2 + 1))
                    if s.has(-4):
                        pool.wait_ge(mix_full, s.mix("pv1").full)
                    for g in range(2):
                        if g or s.has(-1):
                            pool.wait_ge(mix_full, (s.mix("bc0") if g else s.mix("bc1", back=2)).full)
                        settle(pool, settled_pool, s.i)
                        nc.gpsimd.tensor_copy(inv_rows, inv_norm[:, g * H:(g + 1) * H].unsqueeze(2).broadcast_to(
                            [P, H, DK])).then_inc(inv_rows_done, 1)

            over_slots(pool, B, slot)

        @block.scalar
        def _(act):
            act.wait_ge(w_in, 16 * W_LOADS)
            splits = 0
            for u, (kind, dst, part) in enumerate(PREP):
                if kind == "split":
                    act.wait_ge(prep_full, u + 1)
                    nc.scalar.activation(dst[0][:, part, :], prep_bank(u), ACT.Copy).then_inc(prep_hi, 1)
                    splits += 1
            for src, _, dst in st_l:
                nc.scalar.activation(dst[0][:, :, :], src, ACT.Copy).then_inc(lw_hi, 1)

            act.wait_ge(lw_done, 4)

            def exp_rows(src, dst, neg, sums, heads, last):
                for h in range(heads):
                    done = nc.scalar.activation(dst[:, h, :], src(h), ACT.Exp, bias=neg[:, h:h + 1], scale=SCALE,
                                                accum_out=sums[:, h:h + 1])
                done.then_inc(last, 1)

            def copy_proj(s, name, dst, bias):
                u = s.proj(name)
                act.wait_ge(proj_full, u.full)
                ins = nc.scalar.activation(dst, proj_ps[:, u.bank, 0:2 * P], ACT.Identity, bias=bias)
                ins.then_inc(proj_out[u.bank], 1)

            def copy_bd(s, name, dst, c, bias):
                u = s.proj(name)
                act.wait_ge(proj_full, u.full)
                for a in range(2):
                    r = slice(a * DK, (a + 1) * DK)
                    src = proj_ps[r, u.bank, 0:2 * P].rearrange("p (g n) -> p g n", g=2)
                    if bias is None:
                        ins = nc.scalar.activation(dst[r, c, :, a, :], src, ACT.Copy)
                    else:
                        ins = nc.scalar.activation(dst[r, c, :, a, :], src, ACT.Identity, bias=bias[r, c:c + 1])
                ins.then_inc(proj_out[u.bank], 1)

            def hi_part(s, name, dst):
                u = s.mix(name)
                act.wait_ge(mix_full, u.full)
                width = dst.shape[1] * dst.shape[2]
                nc.scalar.activation(dst, mix_ps[:, u.bank, 0:width].rearrange("p (c n) -> p c n", n=P),
                                     ACT.Copy).then_inc(hi_done, 1)

            def slot(s):
                if s.has(-4):
                    u = s.mix("s1")
                    act.wait_ge(neg_lmx_done, s.at(lambda t: t - 4 + 1))
                    if s.has(-5):
                        act.wait_ge(mix_full, s.mix("p1t", back=1).full)
                    exp_rows(lambda h: mix_ps[:, u.bank, h * P:(h + 1) * P], p1_sb, neg_lmx, lsum, H1, mix_out[u.bank])
                if s.has(0):
                    act.wait_ge(neg_mx_done, s.at(lambda t: t + 1))
                    wait(act, ect_full, s.at(lambda t: t))
                    wait(act, den_done, s.at(lambda t: t - 1))
                    exp_rows(lambda h: s_ps[:, h // 4, h % 4, :], e_sb, neg_mx, row_sum[:, s.n % 2, :], H, e_done)
                if not s.odd and s.has(2):
                    for c in (2, 3):
                        copy_proj(s, f"m{c}", m_sb[:, c, :], col_map_b[:, c:c + 1])
                if s.odd and s.has(1):
                    for c in (2, 3):
                        copy_proj(s, f"q{c}", q_t[:, c, :], bias_q[:, c:c + 1])
                if s.has(0):
                    act.wait_ge(ect_full, s.at(lambda t: t + 1))
                    wait(act, av_full, s.at(lambda t: t))
                    nc.scalar.activation(ec_t[:, 0:4, :], s_ps[:, 0], ACT.Copy).then_inc(ect_act, 1)
                if s.odd and s.has(1):
                    copy_bd(s, "k1", k_bd, 1, bias_k)
                if s.has(-4):
                    u = s.mix("p1t")
                    act.wait_ge(mix_full, u.full)
                    nc.scalar.activation(p1_t[:, :, :], mix_ps[:, u.bank, :].rearrange("p (h n) -> p h n", h=H1),
                                         ACT.Copy).then_inc(mix_out[u.bank], 1)
                if not s.odd and s.has(-1):
                    u = s.proj("v1b")
                    act.wait_ge(proj_full, u.full)
                    nc.scalar.activation(lv_sb[:, (s.n - 1) % 4, :], proj_ps[:, u.bank, 0:INNER],
                                         ACT.Copy).then_inc(proj_out[u.bank], 1)
                if s.odd and s.has(1):
                    copy_bd(s, "k3", k_bd, 3, bias_k)
                if s.has(-4):
                    hi_part(s, "pv1", o_t[0][:, :, :])
                if not s.odd and s.has(4):
                    act.wait_ge(ln0_step, s.at(lambda t: 4 * ((t + 4) // 2 + 1)))
                    if s.has(2):
                        act.wait_ge(mix_full, s.mix("ht1", back=1).full)
                    for a in range(2):
                        act.wait_ge(x_in[a], s.at(lambda t: 16 * ((t + 4) // 2 + 1)))
                        nc.scalar.activation(hbuf[:, a, :], xa[:, a, :], ACT.Relu, bias=shift0[:, a:a + 1],
                                             scale=rstd0[:, a:a + 1]).then_inc(h_done, 1)
                if s.odd and s.has(-3):
                    u = s.proj("lq0")
                    act.wait_ge(proj_full, u.full)
                    nc.scalar.activation(lq_t[:, 0, :], proj_ps[:, u.bank, 0:2 * P], ACT.Copy).then_inc(proj_out[u.bank], 1)
                    u = s.proj("lq1")
                    act.wait_ge(proj_full, u.full)
                    nc.scalar.activation(lq_t[:, 1, :], proj_ps[:, u.bank, 0:2 * P], ACT.Copy).then_inc(proj_out[u.bank], 1)
                if s.has(0):
                    act.wait_ge(ln1_step, s.at(lambda t: 4 * (t + 1)))
                    if s.has(-2):
                        name, back = ("h1t1", 2) if s.odd else ("h1t0", 1)
                        act.wait_ge(mix_full, s.mix(name, back=back).full)
                    nc.scalar.activation(hbuf[:, 2 + s.n % 2, :], x1[:, s.n % 4, :], ACT.Relu, bias=shift1[:, 0:1],
                                         scale=rstd1[:, 0:1]).then_inc(h1_done, 1)
                if s.odd and s.has(-3):
                    copy_bd(s, "lk1", lk_bd, 1, None)
                if s.odd and s.has(3):
                    for a in range(2):
                        hi_part(s, f"ht{a}", h_t[0][:, :, a * P:(a + 1) * P])
                if s.odd and s.has(-1):
                    for a in range(2):
                        hi_part(s, f"h1t{a}", h1_t[0][:, :, a * P:(a + 1) * P])

            over_slots(act, B, slot)

        @block.vector
        def _(dve):
            dve.wait_ge(w_in, 16 * W_LOADS)
            splits = 0
            for u, (kind, dst, part) in enumerate(PREP):
                dve.wait_ge(prep_full, u + 1)
                ps = prep_bank(u)
                if kind == "split":
                    splits += 1
                    dve.wait_ge(prep_hi, splits)
                    ins = nc.vector.tensor_tensor(dst[1][:, part, :], ps, dst[0][:, part, :].bitcast(F32), ALU.subtract)
                elif kind == "turn":
                    ins = nc.vector.tensor_copy(st_t[:, part, :], ps)
                elif kind == "bias":
                    ins = nc.vector.tensor_tensor(dst[:, :], ps[:, 0:C], part[:, :], ALU.add)
                elif kind == "gcn":
                    ins = nc.vector.tensor_copy(gcn_bd_t[:, :], ps[:, 0:P])
                else:
                    ins = nc.vector.tensor_copy(bias_v[:, :], ps)
                ins.then_inc(prep_copied, 1)
            for n, (src, _, dst) in enumerate(st_l):
                dve.wait_ge(lw_hi, n + 1)
                nc.vector.tensor_tensor(dst[1][:, :, :], src, dst[0][:, :, :].bitcast(F32), ALU.subtract).then_inc(lw_done, 1)
            dve.wait_ge(prep_copied, len(PREP))
            nc.vector.memset(dir_bd[:, :, :, :, :], 0.0).then_inc(ones_in, 1)
            nc.vector.memset(k_bd[:, :, :, :, :], 0.0).then_inc(ones_in, 1)
            nc.vector.memset(lk_bd[:, :, :, :, :], 0.0).then_inc(ones_in, 1)
            nc.vector.memset(v_sb[:, :, :, DK:DK + 1], 1.0).then_inc(ones_in, 1)
            dve.wait_ge(ones_in, 4)
            dve.wait_ge(lw_done, 4)

            def max_rows(src, mxs, neg, mx_sem, neg_sem, count):
                nc.vector.tensor_reduce(mxs[:, :], src, AX_X, ALU.max).then_inc(mx_sem, 1)
                dve.wait_ge(mx_sem, count)
                nc.vector.tensor_scalar(neg[:, :], mxs[:, :], -SCALE, None, ALU.mult).then_inc(neg_sem, 1)

            def copy_proj(s, name, dst, bias):
                u = s.proj(name)
                dve.wait_ge(proj_full, u.full)
                nc.vector.tensor_scalar(dst, proj_ps[:, u.bank, 0:2 * P], bias, None, ALU.add).then_inc(proj_out[u.bank], 1)

            def copy_bd(s, name, dst, c, bias):
                u = s.proj(name)
                dve.wait_ge(proj_full, u.full)
                for a in range(2):
                    r = slice(a * DK, (a + 1) * DK)
                    src = proj_ps[r, u.bank, 0:2 * P].rearrange("p (g n) -> p g n", g=2)
                    if bias is None:
                        ins = nc.vector.tensor_copy(dst[r, c, :, a, :], src)
                    else:
                        ins = nc.vector.tensor_scalar(dst[r, c, :, a, :], src, bias[r, c:c + 1], None, ALU.add)
                ins.then_inc(proj_out[u.bank], 1)

            def lo_part(s, name, dst, hi):
                u = s.mix(name)
                dve.wait_ge(mix_full, u.full)
                dve.wait_ge(hi_done, s.hi_parts(name))
                width = dst.shape[1] * dst.shape[2]
                nc.vector.tensor_tensor(dst, mix_ps[:, u.bank, 0:width].rearrange("p (c n) -> p c n", n=P),
                                        hi.bitcast(F32), ALU.subtract).then_inc(mix_out[u.bank], 1)

            def v_rows(s, name, ahead):
                u = s.proj(name)
                dve.wait_ge(proj_full, u.full)
                nc.vector.tensor_tensor(v_sb[:, (s.n + ahead) % 4, :, 0:DK],
                                        proj_ps[:, u.bank, :].rearrange("p (h d) -> p h d", h=H),
                                        bias_v[:, :].rearrange("p (h d) -> p h d", h=H),
                                        ALU.add).then_inc(proj_out[u.bank], 1)

            def slot(s):
                if s.has(-4):
                    u = s.mix("s1")
                    dve.wait_ge(mix_full, u.full)
                    max_rows(mix_ps[:, u.bank, :].rearrange("p (h n) -> p h n", h=H1), lmx, neg_lmx, lmx_done,
                             neg_lmx_done, s.at(lambda t: t - 4 + 1))
                if s.has(0):
                    dve.wait_ge(s_full, s.at(lambda t: t + 1))
                    max_rows(s_ps[:, :, :, :].rearrange("p a b n -> p (a b) n"), mx, neg_mx, mx_done, neg_mx_done,
                             s.at(lambda t: t + 1))
                if not s.odd and s.has(2):
                    for c in (0, 1):
                        copy_proj(s, f"m{c}", m_sb[:, c, :], col_map_b[:, c:c + 1])
                if s.odd and s.has(1):
                    for c in (0, 1):
                        copy_proj(s, f"q{c}", q_t[:, c, :], bias_q[:, c:c + 1])
                if s.has(-4):
                    u = s.mix("s1")
                    dve.wait_ge(mix_out[u.bank], u.before + 1)
                    nc.vector.reciprocal(inv_lsum[:, :], lsum[:, :]).then_inc(inv_lsum_done, 1)
                    dve.wait_ge(inv_lsum_done, s.at(lambda t: t - 4 + 1))
                    nc.vector.tensor_tensor(p1_sb[:, :, :], p1_sb[:, :, :],
                                            inv_lsum[:, :].unsqueeze(2).broadcast_to([P, H1, P]),
                                            ALU.mult).then_inc(p1_done, 1)
                if s.has(0):
                    dve.wait_ge(e_done, s.at(lambda t: t + 1))
                    dve.wait_ge(c_full, s.at(lambda t: t + 1))
                    nc.vector.scalar_tensor_tensor(
                        out=e_sb[:, :, :], in0=c_ps[:, :, :].rearrange("p a (b n) -> p (a b) n", b=4), scalar=THRESHOLD,
                        in1=e_sb[:, :, :], op0=ALU.is_gt, op1=ALU.mult).then_inc(ec_done, 1)
                if s.odd and s.has(1):
                    u = s.mix("norm")
                    dve.wait_ge(mix_full, u.full)
                    wait(dve, inv_norm_done, s.at(lambda t: (t + 1) // 2))
                    nc.vector.tensor_scalar(sq_sum[:, :], mix_ps[:, u.bank, 0:2 * H], COS_EPS * COS_EPS, None,
                                            ALU.max).then_inc(mix_out[u.bank], 1)
                if s.has(0):
                    dve.wait_ge(ect_full, s.at(lambda t: t + 1))
                    wait(dve, av_full, s.at(lambda t: t))
                    nc.vector.tensor_copy(ec_t[:, 4:8, :], s_ps[:, 1]).then_inc(ect_dve, 1)
                if s.odd and s.has(1):
                    copy_bd(s, "k0", k_bd, 0, bias_k)
                if not s.odd and s.has(-2):
                    u = s.proj("v1a")
                    dve.wait_ge(proj_full, u.full)
                    nc.vector.tensor_copy(lv_sb[:, (s.n - 2) % 4, :], proj_ps[:, u.bank, 0:INNER]).then_inc(proj_out[u.bank], 1)
                if not s.odd and s.has(4):
                    for a in range(2):
                        dve.wait_ge(x_in[a], s.at(lambda t: 16 * ((t + 4) // 2 + 1)))
                        nc.vector.bn_stats(stats0[:, a, :], xa[:, a, :]).then_inc(stats0_done, 1)
                    wait(dve, ln0_step, s.at(lambda t: 4 * ((t + 4) // 2)))
                    for a in range(2):
                        dve.wait_ge(stats0_done, s.at(lambda t: t + 4 + 2) if a else s.at(lambda t: t + 4 + 1))
                        settle(dve, settled_dve, s.i)
                        nc.vector.bn_aggr(mv0[:, a, :], stats0[:, a, :]).then_inc(mv0_done, 1)
                if s.has(0):
                    dve.wait_ge(av_full, s.at(lambda t: t + 1))
                    nc.vector.tensor_tensor(den[:, :].rearrange("p (a h) -> p a h", a=2),
                                            c_ps[:, :, DK:DK + 3 * (DK + 1) + 1:DK + 1],
                                            row_sum[:, s.n % 2, :].rearrange("p (a h) -> p a h", a=2),
                                            ALU.add).then_inc(den_done, 1)
                    dve.wait_ge(den_done, s.at(lambda t: t + 1))
                    nc.vector.reciprocal(inv_den[:, :], den[:, :]).then_inc(inv_den_done, 1)
                    dve.wait_ge(inv_den_done, s.at(lambda t: t + 1))
                    dve.wait_ge(kept, s.at(lambda t: t + 1))
                    nc.vector.tensor_scalar(gain[:, :], inv_den[:, :], keep[:, s.n % 4:s.n % 4 + 1], None,
                                            ALU.mult).then_inc(gain_done, 1)
                    dve.wait_ge(gain_done, s.at(lambda t: t + 1))
                    wait(dve, y_base, s.at(lambda t: t - 4 + 1))
                    for a in range(2):
                        ins = nc.vector.scalar_tensor_tensor(
                            out=x1[:, s.n % 4, a * D // 2:(a + 1) * D // 2].rearrange("p (h d) -> p h d", h=4),
                            in0=av(a)[:, :, 0:DK], scalar=0.0,
                            in1=gain[:, 4 * a:4 * a + 4].unsqueeze(2).broadcast_to([P, 4, DK]),
                            op0=ALU.max, op1=ALU.mult)
                    ins.then_inc(av_scaled, 1)
                    dve.wait_ge(av_scaled, s.at(lambda t: t + 1))
                    dve.wait_ge(xres_in, s.at(lambda t: 16 * (t + 1)))
                    nc.vector.tensor_tensor(x1[:, s.n % 4, :], x1[:, s.n % 4, :], xres[:, :], ALU.add).then_inc(x1_done, 1)
                    dve.wait_ge(x1_done, s.at(lambda t: t + 1))
                    nc.vector.bn_stats(stats1[:, :], x1[:, s.n % 4, :]).then_inc(stats1_done, 1)
                    dve.wait_ge(stats1_done, s.at(lambda t: t + 1))
                    wait(dve, ln1_step, s.at(lambda t: 4 * t))
                    settle(dve, settled_dve, s.i)
                    nc.vector.bn_aggr(mv1[:, :], stats1[:, :]).then_inc(mv1_done, 1)
                if s.odd and s.has(1):
                    copy_bd(s, "k2", k_bd, 2, bias_k)
                if not s.odd and s.has(2):
                    v_rows(s, "va", 2)
                if s.has(-4):
                    lo_part(s, "pv1", o_t[1][:, :, :], o_t[0][:, :, :])
                if not s.odd and s.has(3):
                    v_rows(s, "vb", 3)
                if s.has(-4):
                    u = s.proj("wo")
                    dve.wait_ge(proj_full, u.full)
                    dve.wait_ge(y_base, s.at(lambda t: t - 4 + 1))
                    nc.vector.tensor_tensor(ybuf[:, s.n % 2, :], proj_ps[:, u.bank, :], ybuf[:, s.n % 2, :],
                                            ALU.add).then_inc(proj_out[u.bank], 1)
                if s.odd and s.has(1):
                    for g in range(2):
                        u = s.mix(f"bc{g}")
                        dve.wait_ge(mix_full, u.full)
                        inv = mix_ps[:, u.bank, :].rearrange("p (c n) -> p c n", c=C)
                        cols = slice(g * P, (g + 1) * P)
                        nc.vector.tensor_tensor(dir_t[:, :, cols], m_sb[:, :, cols], inv, ALU.mult)
                        for a in range(2):
                            r = slice(a * DK, (a + 1) * DK)
                            ins = nc.vector.tensor_tensor(dir_bd[r, :, g, a, :], m_sb[r, :, cols], inv[r], ALU.mult)
                        ins.then_inc(mix_out[u.bank], 1)
                if s.odd and s.has(-3):
                    copy_bd(s, "lk0", lk_bd, 0, None)
                if s.odd and s.has(3):
                    for a in range(2):
                        cols = slice(a * P, (a + 1) * P)
                        lo_part(s, f"ht{a}", h_t[1][:, :, cols], h_t[0][:, :, cols])
                if s.odd and s.has(-1):
                    for a in range(2):
                        cols = slice(a * P, (a + 1) * P)
                        lo_part(s, f"h1t{a}", h1_t[1][:, :, cols], h1_t[0][:, :, cols])

            over_slots(dve, B, slot)

        @block.tensor
        def _(pe):
            def three_passes(ps, w, w_part, mv, mv_part):
                passes = [(c, a, b) for c in range(w[0].shape[1]) for a, b in ((0, 0), (0, 1), (1, 0))]
                for n, (c, a, b) in enumerate(passes):
                    ins = nc.tensor.matmul(ps, w[a][:, c, w_part], mv[b][:, c, mv_part],
                                           start=n == 0, stop=n == len(passes) - 1)
                return ins

            pe.wait_ge(w_in, 16 * W_LOADS)
            pe.wait_ge(consts, 9)
            everything = slice(0, D)
            for u, (kind, dst, part) in enumerate(PREP):
                ps = prep_bank(u)
                needs = u if kind in ("bias",) or (kind == "split" and dst is not w_m) and part == 0 else u - 3
                wait(pe, prep_copied, needs)
                cols = slice(part * P, (part + 1) * P) if isinstance(part, int) else None
                if kind == "split" and dst is w_m:
                    for c in range(C):
                        ins = nc.tensor.transpose(ps[:, c * P:(c + 1) * P], st_map[:, c, cols], ident[:, :])
                elif kind == "turn":
                    for c in range(C):
                        ins = nc.tensor.transpose(ps[:, c * P:(c + 1) * P], dst[:, c, cols], ident[:, :])
                elif kind == "split" and dst is w_v:
                    for c in range(C):
                        ins = nc.tensor.matmul(ps[:, c * P:(c + 1) * P], st_gcn[:, c, cols], gcn_bd_t[:, :],
                                               start=True, stop=True)
                elif kind == "split":
                    for c in range(C):
                        ins = nc.tensor.matmul(ps, st_map[:, c, cols], st_t[:, c, everything],
                                               start=c == 0, stop=c == C - 1)
                elif kind == "bias":
                    for o in range(C):
                        for c in range(C):
                            ins = nc.tensor.matmul(ps[:, o:o + 1], st_t[:, c, o * P:(o + 1) * P],
                                                   col_map_b[:, c:c + 1], start=c == 0, stop=c == C - 1)
                elif kind == "gcn":
                    ins = nc.tensor.transpose(ps[:, 0:P], gcn_bd[:, :], ident[:, :])
                else:
                    for c in range(C):
                        ins = nc.tensor.matmul(ps[:, c * P:(c + 1) * P], col_gb[:, c:c + 1].broadcast_to([P, P]),
                                               gcn_bd_t[:, :], start=True, stop=True)
                ins.then_inc(prep_full, 1)
            pe.wait_ge(prep_copied, len(PREP))
            pe.wait_ge(lw_done, 4)
            pe.wait_ge(ones_in, 4)

            def start_proj(s, name):
                u = s.proj(name)
                wait(pe, proj_out[u.bank], u.before)
                return proj_ps[:, u.bank]

            def start_mix(s, name):
                u = s.mix(name)
                wait(pe, mix_out[u.bank], u.before)
                return mix_ps[:, u.bank]

            both = slice(0, 2 * P)

            def features(s, name, w, c, h):
                ps = start_proj(s, name)
                three_passes(ps[:, 0:2 * P], w, slice(c * P, (c + 1) * P), h, both).then_inc(proj_full, 1)

            def rows(s, name, w, width, h, g):
                ps = start_proj(s, name)
                three_passes(ps[:, 0:width], h, slice(g * P, (g + 1) * P), w, slice(0, width)).then_inc(proj_full, 1)

            def turn(s, name, src):
                ps = start_mix(s, name)
                for c in range(C):
                    ins = nc.tensor.transpose(ps[:, c * P:(c + 1) * P], src[:, c * P:(c + 1) * P], ident[:, :])
                ins.then_inc(mix_full, 1)

            def spread_inv_norm(s, g):
                pe.wait_ge(inv_rows_done, s.at(lambda t: t + 2 + g))
                ps = start_mix(s, f"bc{g}")
                for c in range(C):
                    ins = nc.tensor.transpose(ps[:, c * P:(c + 1) * P],
                                              p1_t[:, c, :], ident[:, :])
                ins.then_inc(mix_full, 1)

            def l1_scores(s):
                if not s.odd:
                    u = s.proj("lk1", back=1)
                    pe.wait_ge(proj_out[u.bank], u.before + 1)
                    u = s.proj("lk0", back=1)
                    pe.wait_ge(proj_out[u.bank], u.before + 1)
                pe.wait_ge(blocked1, s.at(lambda t: t - 4 + 1))
                g = s.n % 2
                ps = start_mix(s, "s1")
                nc.tensor.matmul(ps.rearrange("p (h n) -> p h n", h=4), ident_bf[:, :],
                                 block1[:, s.n % 4, :].unsqueeze(1).broadcast_to([P, 4, P]), start=True, stop=False)
                for c in range(C1):
                    ins = nc.tensor.matmul(ps[:, c * 2 * P:(c + 1) * 2 * P], lq_t[:, c, g * P:(g + 1) * P],
                                           lk_bd[:, c, g, :, :], start=False, stop=c == C1 - 1)
                ins.then_inc(mix_full, 1)

            def scores(s):
                if not s.odd:
                    for c in (2, 3):
                        u = s.proj(f"k{c}", back=1)
                        pe.wait_ge(proj_out[u.bank], u.before + 1)
                pe.wait_ge(blocked0, s.at(lambda t: t + 1))
                wait(pe, ect_act, s.at(lambda t: t))
                wait(pe, ect_dve, s.at(lambda t: t))
                g = s.n % 2
                for a in range(2):
                    nc.tensor.matmul(s_ps[:, a], ident_bf[:, :],
                                     block0[:, s.n % 2, :].unsqueeze(1).broadcast_to([P, 4, P]), start=True, stop=False)
                    for c in range(2):
                        ins = nc.tensor.matmul(s_ps[:, a, 2 * c:2 * c + 2, :], q_t[:, 2 * a + c, g * P:(g + 1) * P],
                                               k_bd[:, 2 * a + c, g, :, :], start=False, stop=c == 1)
                ins.then_inc(s_full, 1)

            def cosines(s):
                if not s.odd:
                    u = s.mix("bc1", back=1)
                    pe.wait_ge(mix_out[u.bank], u.before + 1)
                wait(pe, av_scaled, s.at(lambda t: t))
                g = s.n % 2
                for c in range(C):
                    ins = nc.tensor.matmul(c_ps[:, c // 2, c % 2 * 2 * P:(c % 2 + 1) * 2 * P],
                                           dir_t[:, c, g * P:(g + 1) * P], dir_bd[:, c, g, :, :], start=True, stop=True)
                ins.then_inc(c_full, 1)

            def turn_e(s):
                pe.wait_ge(ec_done, s.at(lambda t: t + 1))
                for h in range(H):
                    ins = nc.tensor.transpose(s_ps[:, h // 4, h % 4, :], e_sb[:, h, :], ident[:, :])
                ins.then_inc(ect_full, 1)

            def weighted_sums(s):
                pe.wait_ge(ect_act, s.at(lambda t: t + 1))
                pe.wait_ge(ect_dve, s.at(lambda t: t + 1))
                for h in range(H):
                    ins = nc.tensor.matmul(av(h // 4)[:, h % 4, :], ec_t[:, h, :], v_sb[:, s.n % 4, h, :],
                                           start=True, stop=True)
                ins.then_inc(av_full, 1)

            def turn_p1(s):
                pe.wait_ge(p1_done, s.at(lambda t: t - 4 + 1))
                ps = start_mix(s, "p1t")
                for h in range(H1):
                    ins = nc.tensor.transpose(ps[:, h * P:(h + 1) * P], p1_sb[:, h, :], ident[:, :])
                ins.then_inc(mix_full, 1)

            def l1_sums(s):
                u = s.mix("p1t")
                pe.wait_ge(mix_out[u.bank], u.before + 1)
                ps = start_mix(s, "pv1")
                for h in range(H1):
                    r = h % 2 * DH
                    ins = nc.tensor.matmul(ps[r:r + DH, h // 2 * P:(h // 2 + 1) * P],
                                           lv_sb[:, s.n % 4, h * DH:(h + 1) * DH], p1_t[:, h, :], start=True, stop=True)
                ins.then_inc(mix_full, 1)

            def output(s):
                u = s.mix("pv1")
                pe.wait_ge(mix_out[u.bank], u.before + 1)
                ps = start_proj(s, "wo")
                three_passes(ps, o_t, slice(0, P), w_o, everything).then_inc(proj_full, 1)

            def slot(s):
                if s.has(-4):
                    l1_scores(s)
                if s.has(0):
                    scores(s)
                    cosines(s)
                if s.odd:
                    if s.has(1):
                        features(s, "q0", w_q, 0, h_t)
                        features(s, "q1", w_q, 1, h_t)
                        features(s, "q2", w_q, 2, h_t)
                        features(s, "q3", w_q, 3, h_t)
                        pe.wait_ge(squared, s.at(lambda t: (t + 1) // 2 + 1))
                        ps = start_mix(s, "norm")
                        for g in range(2):
                            for c in range(C):
                                ins = nc.tensor.matmul(ps[:, g * H:(g + 1) * H], dir_t[:, c, g * P:(g + 1) * P],
                                                       head_sel[:, c, :], start=c == 0, stop=c == C - 1)
                        ins.then_inc(mix_full, 1)
                    if s.has(0):
                        turn_e(s)
                    if s.has(1):
                        features(s, "k0", w_k, 0, h_t)
                        features(s, "k1", w_k, 1, h_t)
                    if s.has(-4):
                        turn_p1(s)
                    if s.has(0):
                        weighted_sums(s)
                    if s.has(1):
                        features(s, "k2", w_k, 2, h_t)
                        features(s, "k3", w_k, 3, h_t)
                    if s.has(-4):
                        l1_sums(s)
                    if s.has(-3):
                        features(s, "lq0", w_lq, 0, h1_t)
                        features(s, "lq1", w_lq, 1, h1_t)
                    if s.has(-4):
                        output(s)
                    if s.has(1):
                        spread_inv_norm(s, 0)
                    if s.has(-3):
                        features(s, "lk0", w_lk, 0, h1_t)
                        features(s, "lk1", w_lk, 1, h1_t)
                    if s.has(1):
                        spread_inv_norm(s, 1)
                    if s.has(3):
                        pe.wait_ge(h_done, s.at(lambda t: t + 5))
                        for g in range(2):
                            turn(s, f"ht{g}", hbuf[:, g, :])
                    if s.has(-1):
                        pe.wait_ge(h1_done, s.at(lambda t: t + 1))
                        for g in range(2):
                            turn(s, f"h1t{g}", hbuf[:, 2 + g, :])
                else:
                    if s.has(2):
                        u = s.mix("ht1", back=1)
                        pe.wait_ge(mix_out[u.bank], u.before + 1)
                        for c in range(C):
                            features(s, f"m{c}", w_m, c, h_t)
                    if s.has(0):
                        turn_e(s)
                    if s.has(-2):
                        u = s.mix("h1t1", back=1)
                        pe.wait_ge(mix_out[u.bank], u.before + 1)
                        rows(s, "v1a", w_lv, INNER, h1_t, 0)
                        rows(s, "v1b", w_lv, INNER, h1_t, 1)
                    if s.has(-4):
                        turn_p1(s)
                    if s.has(0):
                        weighted_sums(s)
                    if s.has(2):
                        rows(s, "va", w_v, D, h_t, 0)
                    if s.has(-4):
                        l1_sums(s)
                    if s.has(2):
                        rows(s, "vb", w_v, D, h_t, 1)
                    if s.has(-4):
                        output(s)

            over_slots(pe, B, slot)


def kernel(**inputs):
    import numpy as np
    import concourse.bacc as bacc
    from concourse.bass_utils import run_bass_kernel_spmd

    names = ["x", "adj", "L0_gnn_map_w", "L0_gnn_map_b", "L0_gnn_q_w", "L0_gnn_q_b", "L0_gnn_k_w", "L0_gnn_k_b",
             "L0_gnn_gcn_map_w", "L0_gnn_gcn_map_b", "L0_gnn_gcn_W", "L1_gnn_Wq", "L1_gnn_Wk", "L1_gnn_Wv",
             "L1_gnn_Wo", "L1_gnn_bo"]
    nc = bacc.Bacc("TRN2", target_bir_lowering=False, num_devices=1)
    arrays, args = {}, []
    for name in names:
        a = np.ascontiguousarray(inputs[name])
        arrays[f"in_{name}_dram"] = a
        args.append(nc.dram_tensor(f"in_{name}_dram", a.shape, mybir.dt.from_np(a.dtype), kind="ExternalInput").ap())
    shape = arrays["in_x_dram"].shape
    args.append(nc.dram_tensor("out_dram", shape, F32, kind="ExternalOutput").ap())
    build(nc, *args)
    return run_bass_kernel_spmd(nc, [arrays], core_ids=[0]).results[0]["out_dram"]
```

```python
from contextlib import ExitStack

import concourse.bass as bass
from concourse import mybir

F32 = mybir.dt.float32
F32R = mybir.dt.float32r
BF16 = mybir.dt.bfloat16
F16 = mybir.dt.float16
U8 = mybir.dt.uint8
ALU = mybir.AluOpType
ACT = mybir.ActivationFunctionType
AX_X = mybir.AxisListType.X

P = 128
UNROLL = 4
BLOCKED = 1e30
LN_EPS = 1e-5
COS_EPS = 1e-8
THRESHOLD = 0.1
DIR_SCALE = 256.0

PROJ_UNITS = (
    (("m0", 2), ("m1", 2), ("m2", 2), ("m3", 2), ("v1a", -2), ("v1b", -1), ("va", 2), ("vb", 3), ("wo", -4)),
    (("q0", 1), ("q1", 1), ("q2", 1), ("q3", 1), ("k0", 1), ("k1", 1), ("k2", 1), ("k3", 1),
     ("lq0", -3), ("lq1", -3), ("lk0", -3), ("lk1", -3), ("wo", -4)),
)
MIX_UNITS = (
    (("s1", -4), ("p1t", -4), ("o1", -4), ("o1t", -4)),
    (("s1", -4), ("norm", 1), ("p1t", -4), ("o1", -4), ("ht0", 3), ("o1t", -4), ("ht1", 4), ("bc0", 1),
     ("h1t0", -1), ("bc1", 2), ("h1t1", 0)),
)
SPLIT_UNITS = ("o1t", "ht0", "ht1", "h1t0", "h1t1")


class Unit:

    def __init__(self, bank, before, full):
        self.bank, self.before, self.full = bank, before, full


class Slot:

    def __init__(self, n, i, graphs):
        self.n, self.i, self.graphs = n, i, graphs
        self.odd = n % 2

    def at(self, f):
        if self.i is None:
            return f(self.n)
        rate = f(self.n + UNROLL) - f(self.n)
        assert f(self.n) > 0 or rate == 0
        return f(self.n) + self.i * rate if rate else f(self.n)

    def has(self, ahead):
        return 0 <= self.n + ahead < self.graphs

    def graph(self, ahead):
        return self.at(lambda t: t + ahead)

    def _unit(self, units, name, back):
        def index(t):
            n = 0
            for u in range(FIRST_SLOT, t):
                n += sum(0 <= u + ahead < self.graphs for _, ahead in units[u % 2])
            for what, ahead in units[t % 2]:
                if what == name:
                    return n
                n += 0 <= t + ahead < self.graphs
            raise KeyError(name)

        at = Slot(self.n - back, self.i, self.graphs)
        return Unit(index(at.n) % 2, at.at(lambda t: index(t) // 2), at.at(lambda t: index(t) + 1))

    def hi_parts(self, name):
        def count(t):
            n = 0
            for u in range(FIRST_SLOT, t + 1):
                for what, ahead in MIX_UNITS[u % 2]:
                    n += what in SPLIT_UNITS and 0 <= u + ahead < self.graphs
                    if u == t and what == name:
                        return n
            raise KeyError(name)
        return self.at(count)

    def proj(self, name, back=0):
        return self._unit(PROJ_UNITS, name, back)

    def mix(self, name, back=0):
        return self._unit(MIX_UNITS, name, back)


FIRST_SLOT = -6
LOOP_FROM = 8
MOST_AHEAD = 6


def wait(engine, sem, count):
    if isinstance(count, int) and count <= 0:
        return
    engine.wait_ge(sem, count)


def settle(engine, sem, loop):
    if loop is not None:
        engine.sem_inc(sem, 1)


def over_slots(engine, graphs, body):
    last = graphs + 4
    loops = (graphs - MOST_AHEAD - LOOP_FROM) // UNROLL
    loop_to = LOOP_FROM + UNROLL * loops
    for n in range(FIRST_SLOT, LOOP_FROM):
        body(Slot(n, None, graphs))
    with engine.Fori(0, loops) as i:
        for j in range(UNROLL):
            body(Slot(LOOP_FROM + j, i, graphs))
    for n in range(loop_to, last):
        body(Slot(n, None, graphs))


def build(nc, x, adj, map_w, map_b, q_w, q_b, k_w, k_b, gcn_map_w, gcn_map_b, gcn_W, Wq, Wk, Wv, Wo, bo, out):
    B, S, D = x.shape
    assert S == P and B % UNROLL == 0
    H = D // gcn_W.shape[0]
    DK = D // H
    C = D // P
    INNER = Wq.shape[1]
    DH = 64
    H1 = INNER // DH
    C1 = INNER // P
    SCALE = float(DK) ** -0.5
    assert DK == 64 and DH == 64 and H == 8 and H1 == 4

    with ExitStack() as ctx:
        def sb(name, shape, dt=F32):
            return ctx.enter_context(nc.sbuf_tensor(name, shape, dt))

        def sem(name):
            return ctx.enter_context(nc.semaphore(name))

        w_m = [sb(f"w_m_{s}", [P, C, D], F32R) for s in ("hi", "lo")]
        w_q = [sb(f"w_q_{s}", [P, C, D], F32R) for s in ("hi", "lo")]
        w_k = [sb(f"w_k_{s}", [P, C, D], F32R) for s in ("hi", "lo")]
        w_v = [sb(f"w_v_{s}", [P, C, D], F32R) for s in ("hi", "lo")]
        w_lq = [sb(f"w_lq_{s}", [P, C, INNER], F32R) for s in ("hi", "lo")]
        w_lk = [sb(f"w_lk_{s}", [P, C, INNER], F32R) for s in ("hi", "lo")]
        w_lv = [sb(f"w_lv_{s}", [P, C, INNER], F32R) for s in ("hi", "lo")]
        w_o = [sb(f"w_o_{s}", [P, C1, D], F32R) for s in ("hi", "lo")]
        ident = sb("ident", [P, P])
        head_sel = sb("head_sel", [P, C, H])
        minus_half = sb("minus_half", [P, 2 * H])
        col_map_b = sb("col_map_b", [P, C])
        col_qb = sb("col_qb", [P, C])
        col_kb = sb("col_kb", [P, C])
        col_gb = sb("col_gb", [P, C])
        bias_q = sb("bias_q", [P, C])
        bias_k = sb("bias_k", [P, C])
        bias_v = sb("bias_v", [P, D])
        bias_o = sb("bias_o", [P, D])
        gcn_bd = sb("gcn_bd", [P, P])
        gcn_bd_t = sb("gcn_bd_t", [P, P])
        xa = sb("xa", [P, 2, D])
        xres = sb("xres", [P, D])
        h1_sb = sb("h1_sb", [P, 2, D])
        x1 = sb("x1", [P, 4, D])
        ybuf = sb("ybuf", [P, D])
        adj_in = sb("adj_in", [P, 4, P], U8)
        block1 = sb("block1", [P, 4, P], BF16)
        keep = sb("keep", [P, 4])
        h_t = [sb(f"h_t_{s}", [P, C, 2 * P], F32R) for s in ("hi", "lo")]
        h1_t = [sb(f"h1_t_{s}", [P, C, 2 * P], F32R) for s in ("hi", "lo")]
        m_sb = sb("m_sb", [P, C, 2 * P])
        sq_t = sb("sq_t", [P, C, 2 * P])
        dir_t = sq_t[:, :, :].rearrange("p c n -> p (c n)").bitcast(F16).rearrange("p (s c n) -> p s c n", s=2, c=C)
        dir_bd = sb("dir_bd", [P, 2, C, 2, 2 * P], F16)
        q_t = sb("q_t", [P, C, 2 * P])
        k_bd = sb("k_bd", [P, C, 2, 2, P])
        v_sb = sb("v_sb", [P, 4, H, DK + 1])
        e_ec = sb("e_ec", [P, 2, H, P])
        e_sb, ec_t = e_ec[:, 0], e_ec[:, 1]
        lq_t = sb("lq_t", [P, C1, 2 * P])
        lk_bd = sb("lk_bd", [P, C1, 2, 2, P])
        lv_sb = sb("lv_sb", [P, 4, H1, DH + 1])
        p1_sb = sb("p1_sb", [P, H1, P])
        p1_t = sb("p1_t", [P, H1, P])
        o1_sb = sb("o1_sb", [P, INNER])
        o_t = [sb(f"o_t_{s}", [P, C1, P], F32R) for s in ("hi", "lo")]
        inv_rows = p1_t[:, :, :].rearrange("p h (a d) -> p (h a) d", d=DK)
        stats0 = sb("stats0", [P, 2, 6])
        mv0 = sb("mv0", [P, 2, 2])
        ve0 = sb("ve0", [P, 2])
        nm0 = sb("nm0", [P, 2])
        rstd0 = sb("rstd0", [P, 2])
        shift0 = sb("shift0", [P, 2])
        stats1 = sb("stats1", [P, 6])
        mv1 = sb("mv1", [P, 2])
        ve1 = sb("ve1", [P, 1])
        nm1 = sb("nm1", [P, 1])
        rstd1 = sb("rstd1", [P, 1])
        shift1 = sb("shift1", [P, 1])
        sq_sum = sb("sq_sum", [P, 2 * H])
        inv_norm = sb("inv_norm", [P, 2 * H])
        mx = sb("mx", [P, H])
        neg_mx = sb("neg_mx", [P, H])
        row_sum = sb("row_sum", [P, 2, H])
        den = sb("den", [P, H])
        inv_den = sb("inv_den", [P, H])
        gain = sb("gain", [P, H])
        lmx = sb("lmx", [P, H1])
        neg_lmx = sb("neg_lmx", [P, H1])
        inv_lsum = sb("inv_lsum", [P, H1])

        s_ps = ctx.enter_context(nc.psum_tensor("s_ps", [P, 2, 4, P], F32))
        c_ps = ctx.enter_context(nc.psum_tensor("c_ps", [P, 2, 4 * P], F32))
        proj_ps = ctx.enter_context(nc.psum_tensor("proj_ps", [P, 2, 4 * P], F32))
        mix_ps = ctx.enter_context(nc.psum_tensor("mix_ps", [P, 2, 4 * P], F32))

        def av(a):
            return c_ps[:, a, 0:4 * (DK + 1)].rearrange("p (h d) -> p h d", h=4)

        w_in = sem("w_in")
        consts = sem("consts")
        ones_in = sem("ones_in")
        prep_full = sem("prep_full")
        prep_hi = sem("prep_hi")
        prep_copied = sem("prep_copied")
        lw_hi = sem("lw_hi")
        lw_done = sem("lw_done")
        x_in = [sem(f"x_in{i}") for i in range(2)]
        a_in = [sem(f"a_in{i}") for i in range(4)]
        xres_in = sem("xres_in")
        y_out = sem("y_out")
        proj_full = sem("proj_full")
        proj_out = [sem(f"proj_out{i}") for i in range(2)]
        mix_full = sem("mix_full")
        mix_out = [sem(f"mix_out{i}") for i in range(2)]
        s_full = sem("s_full")
        c_full = sem("c_full")
        ect_full = sem("ect_full")
        av_full = sem("av_full")
        blocked1 = sem("blocked1")
        kept = sem("kept")
        stats0_done = sem("stats0_done")
        mv0_done = sem("mv0_done")
        ln0_step = sem("ln0_step")
        h_done = sem("h_done")
        stats1_done = sem("stats1_done")
        mv1_done = sem("mv1_done")
        ln1_step = sem("ln1_step")
        h1_done = sem("h1_done")
        squared = sem("squared")
        inv_norm_done = sem("inv_norm_done")
        inv_rows_done = sem("inv_rows_done")
        masked = sem("masked")
        mx_done = sem("mx_done")
        neg_mx_done = sem("neg_mx_done")
        e_done = sem("e_done")
        ec_done = sem("ec_done")
        ect_act = sem("ect_act")
        ect_dve = sem("ect_dve")
        den_done = sem("den_done")
        inv_den_done = sem("inv_den_done")
        gain_done = sem("gain_done")
        av_scaled = sem("av_scaled")
        x1_done = sem("x1_done")
        lmx_done = sem("lmx_done")
        neg_lmx_done = sem("neg_lmx_done")
        inv_lsum_done = sem("inv_lsum_done")
        p1_done = sem("p1_done")
        o1_done = sem("o1_done")
        dir_hi = sem("dir_hi")
        dir_lo = sem("dir_lo")
        dir_done = sem("dir_done")
        hi_done = sem("hi_done")
        y_base = sem("y_base")
        settled_sp = sem("settled_sp")
        settled_pool = sem("settled_pool")
        settled_dve = sem("settled_dve")

        st_map, st_q, st_k, st_gcn = (
            x1[:, :, :], e_ec[:, :, :, :].rearrange("p a h n -> p (a h n)").rearrange("p (c n) -> p c n", c=C),
            dir_bd[:, :, :, :, :].rearrange("p s c g n -> p (s c g n)").bitcast(F32).rearrange("p (c n) -> p c n", c=C),
            k_bd[:, :, :, :, :].rearrange("p c g a b -> p c (g a b)"))
        st_t = v_sb[:, :, :, :].rearrange("p a h d -> p (a h d)")[:, 0:C * D].rearrange("p (c n) -> p c n", c=C)
        st_l = [(m_sb[:, :, :], Wq, w_lq), (sq_t[:, :, :], Wk, w_lk),
                (xa[:, :, :].rearrange("p a (c n) -> p (a c) n", c=2), Wv, w_lv), (h1_sb[:, :, :], Wo, w_o)]

        def prep_bank(u):
            return (proj_ps, mix_ps)[u % 4 // 2][:, u % 2]

        PREP = ([("split", w_m, c) for c in range(C)]
                + [("turn", st_q, c) for c in range(C)] + [("split", w_q, c) for c in range(C)] + [("bias", bias_q, col_qb)]
                + [("turn", st_k, c) for c in range(C)] + [("split", w_k, c) for c in range(C)] + [("bias", bias_k, col_kb)]
                + [("gcn", None, 0)] + [("split", w_v, c) for c in range(C)] + [("bias_v", None, 0)])
        W_LOADS = 15

        block = ctx.enter_context(nc.Block())

        @block.sync
        def _(sp):
            for dst, src in ((st_map, map_w), (st_q, q_w), (st_k, k_w), (st_gcn, gcn_map_w)):
                sp.dma_start(dst, src.rearrange("(c p) n -> p c n", p=P)).then_inc(w_in, 16)
            for dst, src, _ in st_l:
                sp.dma_start(dst, src.rearrange("(c p) n -> p c n", p=P)).then_inc(w_in, 16)
            for dst, src in ((col_map_b, map_b), (col_qb, q_b), (col_kb, k_b), (col_gb, gcn_map_b)):
                sp.dma_start(dst[:, :], src.rearrange("(c p) -> p c", p=P),
                             allow_slow_non_contiguous=True).then_inc(w_in, 16)
            sp.dma_start(bias_o[:, :], bo.rearrange("(a n) -> a n", a=1).broadcast_to([P, D])).then_inc(w_in, 16)
            sp.wait_ge(consts, 1)
            for a in range(2):
                sp.dma_start(gcn_bd[a * DK:(a + 1) * DK, a * DK:(a + 1) * DK], gcn_W).then_inc(w_in, 16)

            def slot(s):
                if s.has(3):
                    wait(sp, blocked1, s.at(lambda t: t))
                    wait(sp, masked, s.at(lambda t: t))
                    settle(sp, settled_sp, s.i)
                    sp.dma_start(adj_in[:, (s.n + 3) % 4, :], adj[s.graph(3)]).then_inc(a_in[(s.n + 3) % 4], 16)
                if s.has(0):
                    wait(sp, x1_done, s.at(lambda t: t))
                    settle(sp, settled_sp, s.i)
                    sp.dma_start(xres[:, :], x[s.graph(0)]).then_inc(xres_in, 16)
                if s.odd:
                    for a in range(2):
                        if s.has(5 + a):
                            if s.has(3 + a):
                                sp.wait_ge(mix_full, s.mix(f"ht{a}").full)
                            settle(sp, settled_sp, s.i)
                            sp.dma_start(xa[:, a, :], x[s.graph(5 + a)]).then_inc(x_in[a], 16)
                if s.has(-4):
                    u = s.proj("wo")
                    sp.wait_ge(proj_out[u.bank], u.before + 1)
                    settle(sp, settled_sp, s.i)
                    sp.dma_start(out[s.graph(-4)], ybuf[:, :]).then_inc(y_out, 16)

            sp.wait_ge(lw_done, 4)
            over_slots(sp, B, slot)
            sp.wait_ge(y_out, 16 * B)

        @block.gpsimd
        def _(pool):
            nc.gpsimd.memset(gcn_bd[:, :], 0.0).then_inc(consts, 1)
            nc.gpsimd.memset(ident[:, :], 0.0).then_inc(consts, 1)
            nc.gpsimd.memset(head_sel[:, :, :], 0.0).then_inc(consts, 1)
            nc.gpsimd.memset(minus_half[:, :], -0.5).then_inc(consts, 1)
            pool.wait_ge(consts, 4)
            nc.gpsimd.affine_select(out=ident[:, :], in_=ident[:, :], compare_op=ALU.not_equal, fill=1.0, base=0,
                                    pattern=[[-1, P]], channel_multiplier=1).then_inc(consts, 1)
            flat = head_sel[:, :, :].rearrange("p c h -> p (c h)")
            pool.wait_ge(consts, 5)
            for a in range(2):
                nc.gpsimd.memset(flat[a * DK:(a + 1) * DK, a:a + (C - 1) * (H + 2) + 1:H + 2], 1.0).then_inc(consts, 1)

            def slot(s):
                if s.odd and s.has(1):
                    for c in (2, 3):
                        u = s.proj(f"m{c}", back=1)
                        pool.wait_ge(proj_out[u.bank], u.before + 1)
                    wait(pool, c_full, s.at(lambda t: t + 1))
                    nc.gpsimd.tensor_tensor(sq_t[:, :, :], m_sb[:, :, :], m_sb[:, :, :], ALU.mult).then_inc(squared, 1)
                if s.has(1):
                    r = (s.n + 1) % 4
                    pool.wait_ge(a_in[r], s.at(lambda t: 16 * ((t + 1) // 4 + 1)))
                    wait(pool, x1_done, s.at(lambda t: t - 2))
                    settle(pool, settled_pool, s.i)
                    nc.gpsimd.tensor_scalar(keep[:, r:r + 1], adj_in[:, r, 0:1], -1.0, 1.0, ALU.mult,
                                            ALU.add).then_inc(kept, 1)
                if s.has(0):
                    if s.has(-4):
                        u = s.mix("s1")
                        pool.wait_ge(mix_out[u.bank], u.before + 1)
                    settle(pool, settled_pool, s.i)
                    nc.gpsimd.tensor_scalar(block1[:, s.n % 4, :], adj_in[:, s.n % 4, :], -1.0, BLOCKED, ALU.add,
                                            ALU.mult).then_inc(blocked1, 1)
                if s.has(-4):
                    wait(pool, y_out, s.at(lambda t: 16 * (t - 4)))
                    nc.gpsimd.tensor_tensor(ybuf[:, :], x1[:, s.n % 4, :], bias_o[:, :],
                                            ALU.add).then_inc(y_base, 1)
                if s.odd and s.has(1):
                    u = s.mix("norm")
                    pool.wait_ge(mix_out[u.bank], u.before + 1)
                    nc.gpsimd.tensor_tensor(inv_norm[:, :], sq_sum[:, :], minus_half[:, :], ALU.pow).then_inc(inv_norm_done, 1)
                if not s.odd and s.has(4):
                    before = s.at(lambda t: 4 * ((t + 4) // 2))
                    pool.wait_ge(mv0_done, s.at(lambda t: t + 4 + 2))
                    wait(pool, h_done, s.at(lambda t: t + 4))
                    settle(pool, settled_pool, s.i)
                    nc.gpsimd.tensor_scalar(ve0[:, :], mv0[:, :, 1], LN_EPS, None, ALU.add).then_inc(ln0_step, 1)
                    nc.gpsimd.tensor_scalar(nm0[:, :], mv0[:, :, 0], -1.0, None, ALU.mult).then_inc(ln0_step, 1)
                    pool.wait_ge(ln0_step, before + 2)
                    nc.gpsimd.tensor_tensor(rstd0[:, :], ve0[:, :], minus_half[:, 0:2], ALU.pow).then_inc(ln0_step, 1)
                    pool.wait_ge(ln0_step, before + 3)
                    nc.gpsimd.tensor_tensor(shift0[:, :], nm0[:, :], rstd0[:, :], ALU.mult).then_inc(ln0_step, 1)
                if s.has(0):
                    before = s.at(lambda t: 4 * t)
                    pool.wait_ge(mv1_done, s.at(lambda t: t + 1))
                    wait(pool, h1_done, s.at(lambda t: t))
                    settle(pool, settled_pool, s.i)
                    nc.gpsimd.tensor_scalar(ve1[:, :], mv1[:, 1:2], LN_EPS, None, ALU.add).then_inc(ln1_step, 1)
                    nc.gpsimd.tensor_scalar(nm1[:, :], mv1[:, 0:1], -1.0, None, ALU.mult).then_inc(ln1_step, 1)
                    pool.wait_ge(ln1_step, before + 2)
                    nc.gpsimd.tensor_tensor(rstd1[:, :], ve1[:, :], minus_half[:, 0:1], ALU.pow).then_inc(ln1_step, 1)
                    pool.wait_ge(ln1_step, before + 3)
                    nc.gpsimd.tensor_tensor(shift1[:, :], nm1[:, :], rstd1[:, :], ALU.mult).then_inc(ln1_step, 1)

                if s.odd and s.has(1):
                    pool.wait_ge(inv_norm_done, s.at(lambda t: (t + 1) // 2 + 1))
                    if s.has(-4):
                        pool.wait_ge(mix_full, s.mix("o1").full)
                    for g in range(2):
                        if g or s.has(-1):
                            pool.wait_ge(mix_full, (s.mix("bc0") if g else s.mix("bc1", back=2)).full)
                        settle(pool, settled_pool, s.i)
                        nc.gpsimd.tensor_copy(inv_rows, inv_norm[:, g * H:(g + 1) * H].unsqueeze(2).broadcast_to(
                            [P, H, DK])).then_inc(inv_rows_done, 1)

            over_slots(pool, B, slot)

        @block.scalar
        def _(act):
            act.wait_ge(w_in, 16 * W_LOADS)
            splits = 0
            for u, (kind, dst, part) in enumerate(PREP):
                if kind == "split":
                    act.wait_ge(prep_full, u + 1)
                    nc.scalar.activation(dst[0][:, part, :], prep_bank(u), ACT.Copy).then_inc(prep_hi, 1)
                    splits += 1
            for src, _, dst in st_l:
                nc.scalar.activation(dst[0][:, :, :], src, ACT.Copy).then_inc(lw_hi, 1)

            act.wait_ge(lw_done, 4)

            def exp_rows(e, neg, heads, done, sums=None):
                for h in range(heads):
                    if sums is None:
                        ins = nc.scalar.activation(e[:, h, :], e[:, h, :], ACT.Exp, bias=neg[:, h:h + 1], scale=SCALE)
                    else:
                        ins = nc.scalar.activation(e[:, h, :], e[:, h, :], ACT.Exp, bias=neg[:, h:h + 1], scale=SCALE,
                                                   accum_out=sums[:, h:h + 1])
                ins.then_inc(done, 1)

            def copy_proj(s, name, dst, bias):
                u = s.proj(name)
                act.wait_ge(proj_full, u.full)
                ins = nc.scalar.activation(dst, proj_ps[:, u.bank, 0:2 * P], ACT.Identity, bias=bias)
                ins.then_inc(proj_out[u.bank], 1)

            def copy_bd(s, name, dst, c, bias):
                u = s.proj(name)
                act.wait_ge(proj_full, u.full)
                for a in range(2):
                    r = slice(a * DK, (a + 1) * DK)
                    src = proj_ps[r, u.bank, 0:2 * P].rearrange("p (g n) -> p g n", g=2)
                    if bias is None:
                        ins = nc.scalar.activation(dst[r, c, :, a, :], src, ACT.Copy)
                    else:
                        ins = nc.scalar.activation(dst[r, c, :, a, :], src, ACT.Identity, bias=bias[r, c:c + 1])
                ins.then_inc(proj_out[u.bank], 1)

            def scaled_hi(s, g):
                u = s.mix(f"bc{g}")
                act.wait_ge(mix_out[u.bank], u.before + 1)
                cols = slice(g * P, (g + 1) * P)
                nc.scalar.activation(dir_t[:, 0, :, cols], m_sb[:, :, cols], ACT.Copy).then_inc(dir_hi, 1)

            def hi_part(s, name, dst):
                u = s.mix(name)
                act.wait_ge(mix_full, u.full)
                width = dst.shape[1] * dst.shape[2]
                nc.scalar.activation(dst, mix_ps[:, u.bank, 0:width].rearrange("p (c n) -> p c n", n=P),
                                     ACT.Copy).then_inc(hi_done, 1)

            def slot(s):
                if s.has(-4):
                    act.wait_ge(neg_lmx_done, s.at(lambda t: t - 4 + 1))
                    exp_rows(p1_sb, neg_lmx, H1, p1_done)
                if s.has(0):
                    act.wait_ge(neg_mx_done, s.at(lambda t: t + 1))
                    wait(act, den_done, s.at(lambda t: t - 1))
                    exp_rows(e_sb, neg_mx, H, e_done, row_sum[:, s.n % 2, :])
                if not s.odd and s.has(2):
                    for c in (2, 3):
                        copy_proj(s, f"m{c}", m_sb[:, c, :], col_map_b[:, c:c + 1])
                if s.odd and s.has(1):
                    for c in (2, 3):
                        copy_proj(s, f"q{c}", q_t[:, c, :], bias_q[:, c:c + 1])
                if s.has(0):
                    act.wait_ge(ect_full, s.at(lambda t: t + 1))
                    wait(act, av_full, s.at(lambda t: t))
                    nc.scalar.activation(ec_t[:, 0:4, :], s_ps[:, 0], ACT.Copy).then_inc(ect_act, 1)
                if s.odd and s.has(1):
                    copy_bd(s, "k1", k_bd, 1, bias_k)
                if s.has(-4):
                    u = s.mix("p1t")
                    act.wait_ge(mix_full, u.full)
                    nc.scalar.activation(p1_t[:, :, :], mix_ps[:, u.bank, :].rearrange("p (h n) -> p h n", h=H1),
                                         ACT.Copy).then_inc(mix_out[u.bank], 1)
                if not s.odd and s.has(-1):
                    u = s.proj("v1b")
                    act.wait_ge(proj_full, u.full)
                    nc.scalar.activation(lv_sb[:, (s.n - 1) % 4, :, 0:DH],
                                         proj_ps[:, u.bank, 0:INNER].rearrange("p (h d) -> p h d", h=H1),
                                         ACT.Copy).then_inc(proj_out[u.bank], 1)
                if s.odd and s.has(1):
                    copy_bd(s, "k2", k_bd, 2, bias_k)
                    copy_bd(s, "k3", k_bd, 3, bias_k)
                if s.odd and s.has(3):
                    hi_part(s, "ht0", h_t[0][:, :, 0:P])
                if s.has(-4):
                    hi_part(s, "o1t", o_t[0][:, :, :])
                if s.odd and s.has(4):
                    hi_part(s, "ht1", h_t[0][:, :, P:2 * P])
                if not s.odd and s.has(4):
                    act.wait_ge(ln0_step, s.at(lambda t: 4 * ((t + 4) // 2 + 1)))
                    for a in range(2):
                        act.wait_ge(x_in[a], s.at(lambda t: 16 * ((t + 4) // 2 + 1)))
                        nc.scalar.activation(xa[:, a, :], xa[:, a, :], ACT.Relu, bias=shift0[:, a:a + 1],
                                             scale=rstd0[:, a:a + 1]).then_inc(h_done, 1)
                if s.has(0):
                    act.wait_ge(ln1_step, s.at(lambda t: 4 * (t + 1)))
                    if s.has(-2):
                        name, back = ("h1t1", 2) if s.odd else ("h1t0", 1)
                        act.wait_ge(mix_full, s.mix(name, back=back).full)
                    nc.scalar.activation(h1_sb[:, s.n % 2, :], x1[:, s.n % 4, :], ACT.Relu, bias=shift1[:, 0:1],
                                         scale=rstd1[:, 0:1]).then_inc(h1_done, 1)
                if s.odd and s.has(-3):
                    copy_bd(s, "lk1", lk_bd, 1, None)
                if s.odd and s.has(1):
                    scaled_hi(s, 0)
                if s.odd and s.has(-1):
                    hi_part(s, "h1t0", h1_t[0][:, :, 0:P])
                if s.odd and s.has(2):
                    scaled_hi(s, 1)
                if s.odd and s.has(0):
                    hi_part(s, "h1t1", h1_t[0][:, :, P:2 * P])

            over_slots(act, B, slot)

        @block.vector
        def _(dve):
            dve.wait_ge(w_in, 16 * W_LOADS)
            splits = 0
            for u, (kind, dst, part) in enumerate(PREP):
                dve.wait_ge(prep_full, u + 1)
                ps = prep_bank(u)
                if kind == "split":
                    splits += 1
                    dve.wait_ge(prep_hi, splits)
                    ins = nc.vector.tensor_tensor(dst[1][:, part, :], ps, dst[0][:, part, :].bitcast(F32), ALU.subtract)
                elif kind == "turn":
                    ins = nc.vector.tensor_copy(st_t[:, part, :], ps)
                elif kind == "bias":
                    ins = nc.vector.tensor_tensor(dst[:, :], ps[:, 0:C], part[:, :], ALU.add)
                elif kind == "gcn":
                    ins = nc.vector.tensor_copy(gcn_bd_t[:, :], ps[:, 0:P])
                else:
                    ins = nc.vector.tensor_copy(bias_v[:, :], ps)
                ins.then_inc(prep_copied, 1)
            for n, (src, _, dst) in enumerate(st_l):
                dve.wait_ge(lw_hi, n + 1)
                nc.vector.tensor_tensor(dst[1][:, :, :], src, dst[0][:, :, :].bitcast(F32), ALU.subtract).then_inc(lw_done, 1)
            dve.wait_ge(prep_copied, len(PREP))
            nc.vector.memset(dir_bd[:, :, :, :, :].rearrange("p s c g n -> p (s c g n)").bitcast(F32), 0.0
                             ).then_inc(ones_in, 1)
            nc.vector.memset(k_bd[:, :, :, :, :], 0.0).then_inc(ones_in, 1)
            nc.vector.memset(lk_bd[:, :, :, :, :], 0.0).then_inc(ones_in, 1)
            nc.vector.memset(v_sb[:, :, :, DK:DK + 1], 1.0).then_inc(ones_in, 1)
            nc.vector.memset(lv_sb[:, :, :, DH:DH + 1], 1.0).then_inc(ones_in, 1)
            dve.wait_ge(ones_in, 5)
            dve.wait_ge(lw_done, 4)

            def max_rows(src, mxs, neg, mx_sem, neg_sem, count):
                nc.vector.tensor_reduce(mxs[:, :], src, AX_X, ALU.max).then_inc(mx_sem, 1)
                dve.wait_ge(mx_sem, count)
                nc.vector.tensor_scalar(neg[:, :], mxs[:, :], -SCALE, None, ALU.mult).then_inc(neg_sem, 1)

            def copy_proj(s, name, dst, bias):
                u = s.proj(name)
                dve.wait_ge(proj_full, u.full)
                nc.vector.tensor_scalar(dst, proj_ps[:, u.bank, 0:2 * P], bias, None, ALU.add).then_inc(proj_out[u.bank], 1)

            def copy_bd(s, name, dst, c, bias):
                u = s.proj(name)
                dve.wait_ge(proj_full, u.full)
                for a in range(2):
                    r = slice(a * DK, (a + 1) * DK)
                    src = proj_ps[r, u.bank, 0:2 * P].rearrange("p (g n) -> p g n", g=2)
                    if bias is None:
                        ins = nc.vector.tensor_copy(dst[r, c, :, a, :], src)
                    else:
                        ins = nc.vector.tensor_scalar(dst[r, c, :, a, :], src, bias[r, c:c + 1], None, ALU.add)
                ins.then_inc(proj_out[u.bank], 1)

            def lo_part(s, name, dst, hi):
                u = s.mix(name)
                dve.wait_ge(mix_full, u.full)
                dve.wait_ge(hi_done, s.hi_parts(name))
                width = dst.shape[1] * dst.shape[2]
                nc.vector.tensor_tensor(dst, mix_ps[:, u.bank, 0:width].rearrange("p (c n) -> p c n", n=P),
                                        hi.bitcast(F32), ALU.subtract).then_inc(mix_out[u.bank], 1)

            def v_rows(s, name, ahead):
                u = s.proj(name)
                dve.wait_ge(proj_full, u.full)
                nc.vector.tensor_tensor(v_sb[:, (s.n + ahead) % 4, :, 0:DK],
                                        proj_ps[:, u.bank, :].rearrange("p (h d) -> p h d", h=H),
                                        bias_v[:, :].rearrange("p (h d) -> p h d", h=H),
                                        ALU.add).then_inc(proj_out[u.bank], 1)

            def v1_rows(s, name, ahead):
                u = s.proj(name)
                dve.wait_ge(proj_full, u.full)
                nc.vector.tensor_copy(lv_sb[:, (s.n + ahead) % 4, :, 0:DH],
                                      proj_ps[:, u.bank, 0:INNER].rearrange("p (h d) -> p h d", h=H1)
                                      ).then_inc(proj_out[u.bank], 1)

            def directions(s, g):
                u = s.mix(f"bc{g}")
                cols = slice(g * P, (g + 1) * P)
                dve.wait_ge(mix_full, u.full)
                nc.vector.tensor_tensor(m_sb[:, :, cols], m_sb[:, :, cols],
                                        mix_ps[:, u.bank, :].rearrange("p (c n) -> p c n", c=C),
                                        ALU.mult).then_inc(mix_out[u.bank], 1)

            def direction_blocks(s, g):
                cols = slice(g * P, (g + 1) * P)
                dve.wait_ge(dir_hi, s.at(lambda t: t + 2 + g))
                nc.vector.tensor_tensor(dir_t[:, 1, :, cols], m_sb[:, :, cols], dir_t[:, 0, :, cols],
                                        ALU.subtract).then_inc(dir_lo, 1)
                for a in range(2):
                    r = slice(a * DK, (a + 1) * DK)
                    nc.vector.tensor_copy(dir_bd[r, 0, :, g, a * P:(a + 1) * P], dir_t[r, 0, :, cols])
                dve.wait_ge(dir_lo, s.at(lambda t: t + 2 + g))
                for a in range(2):
                    r = slice(a * DK, (a + 1) * DK)
                    ins = nc.vector.tensor_copy(dir_bd[r, 1, :, g, a * P:(a + 1) * P], dir_t[r, 1, :, cols])
                ins.then_inc(dir_done, 1)

            def slot(s):
                if s.has(-4):
                    u = s.mix("s1")
                    dve.wait_ge(mix_full, u.full)
                    dve.wait_ge(blocked1, s.at(lambda t: t - 4 + 1))
                    if s.has(-5):
                        dve.wait_ge(mix_full, s.mix("p1t", back=1).full)
                    nc.vector.tensor_tensor(p1_sb[:, :, :], mix_ps[:, u.bank, :].rearrange("p (h n) -> p h n", h=H1),
                                            block1[:, s.n % 4, :].unsqueeze(1).broadcast_to([P, H1, P]),
                                            ALU.add).then_inc(mix_out[u.bank], 1)
                    dve.wait_ge(mix_out[u.bank], u.before + 1)
                    max_rows(p1_sb[:, :, :], lmx, neg_lmx, lmx_done, neg_lmx_done, s.at(lambda t: t - 4 + 1))
                if s.has(0):
                    dve.wait_ge(s_full, s.at(lambda t: t + 1))
                    dve.wait_ge(a_in[s.n % 4], s.at(lambda t: 16 * (t // 4 + 1)))
                    wait(dve, ect_full, s.at(lambda t: t))
                    nc.vector.scalar_tensor_tensor(
                        out=e_sb[:, :, :], in0=adj_in[:, s.n % 4, :].unsqueeze(1).broadcast_to([P, H, P]),
                        scalar=-BLOCKED, in1=s_ps[:, :, :, :].rearrange("p a b n -> p (a b) n"),
                        op0=ALU.mult, op1=ALU.add).then_inc(masked, 1)
                    dve.wait_ge(masked, s.at(lambda t: t + 1))
                    max_rows(e_sb[:, :, :], mx, neg_mx, mx_done, neg_mx_done, s.at(lambda t: t + 1))
                if not s.odd and s.has(2):
                    for c in (0, 1):
                        copy_proj(s, f"m{c}", m_sb[:, c, :], col_map_b[:, c:c + 1])
                if s.odd and s.has(1):
                    for c in (0, 1):
                        copy_proj(s, f"q{c}", q_t[:, c, :], bias_q[:, c:c + 1])
                if s.has(0):
                    dve.wait_ge(e_done, s.at(lambda t: t + 1))
                    dve.wait_ge(c_full, s.at(lambda t: t + 1))
                    nc.vector.scalar_tensor_tensor(
                        out=e_sb[:, :, :], in0=c_ps[:, :, :].rearrange("p a (b n) -> p (a b) n", b=4),
                        scalar=THRESHOLD * DIR_SCALE * DIR_SCALE, in1=e_sb[:, :, :], op0=ALU.is_gt,
                        op1=ALU.mult).then_inc(ec_done, 1)
                if s.odd and s.has(1):
                    u = s.mix("norm")
                    dve.wait_ge(mix_full, u.full)
                    wait(dve, inv_norm_done, s.at(lambda t: (t + 1) // 2))
                    nc.vector.tensor_scalar(sq_sum[:, :], mix_ps[:, u.bank, 0:2 * H], COS_EPS * COS_EPS,
                                            1.0 / (DIR_SCALE * DIR_SCALE), ALU.max, ALU.mult).then_inc(mix_out[u.bank], 1)
                if s.has(0):
                    dve.wait_ge(ect_full, s.at(lambda t: t + 1))
                    wait(dve, av_full, s.at(lambda t: t))
                    nc.vector.tensor_copy(ec_t[:, 4:8, :], s_ps[:, 1]).then_inc(ect_dve, 1)
                if s.odd and s.has(1):
                    copy_bd(s, "k0", k_bd, 0, bias_k)
                if not s.odd and s.has(-2):
                    v1_rows(s, "v1a", -2)
                if not s.odd and s.has(4):
                    for a in range(2):
                        dve.wait_ge(x_in[a], s.at(lambda t: 16 * ((t + 4) // 2 + 1)))
                        nc.vector.bn_stats(stats0[:, a, :], xa[:, a, :]).then_inc(stats0_done, 1)
                    wait(dve, ln0_step, s.at(lambda t: 4 * ((t + 4) // 2)))
                    for a in range(2):
                        dve.wait_ge(stats0_done, s.at(lambda t: t + 4 + 2) if a else s.at(lambda t: t + 4 + 1))
                        settle(dve, settled_dve, s.i)
                        nc.vector.bn_aggr(mv0[:, a, :], stats0[:, a, :]).then_inc(mv0_done, 1)
                if s.has(0):
                    dve.wait_ge(av_full, s.at(lambda t: t + 1))
                    nc.vector.tensor_tensor(den[:, :].rearrange("p (a h) -> p a h", a=2),
                                            c_ps[:, :, DK:DK + 3 * (DK + 1) + 1:DK + 1],
                                            row_sum[:, s.n % 2, :].rearrange("p (a h) -> p a h", a=2),
                                            ALU.add).then_inc(den_done, 1)
                    dve.wait_ge(den_done, s.at(lambda t: t + 1))
                    nc.vector.reciprocal(inv_den[:, :], den[:, :]).then_inc(inv_den_done, 1)
                    dve.wait_ge(inv_den_done, s.at(lambda t: t + 1))
                    dve.wait_ge(kept, s.at(lambda t: t + 1))
                    nc.vector.tensor_scalar(gain[:, :], inv_den[:, :], keep[:, s.n % 4:s.n % 4 + 1], None,
                                            ALU.mult).then_inc(gain_done, 1)
                    dve.wait_ge(gain_done, s.at(lambda t: t + 1))
                    wait(dve, y_base, s.at(lambda t: t - 4 + 1))
                    for a in range(2):
                        ins = nc.vector.scalar_tensor_tensor(
                            out=x1[:, s.n % 4, a * D // 2:(a + 1) * D // 2].rearrange("p (h d) -> p h d", h=4),
                            in0=av(a)[:, :, 0:DK], scalar=0.0,
                            in1=gain[:, 4 * a:4 * a + 4].unsqueeze(2).broadcast_to([P, 4, DK]),
                            op0=ALU.max, op1=ALU.mult)
                    ins.then_inc(av_scaled, 1)
                    dve.wait_ge(av_scaled, s.at(lambda t: t + 1))
                    dve.wait_ge(xres_in, s.at(lambda t: 16 * (t + 1)))
                    nc.vector.tensor_tensor(x1[:, s.n % 4, :], x1[:, s.n % 4, :], xres[:, :], ALU.add).then_inc(x1_done, 1)
                if s.has(-4):
                    u = s.mix("o1")
                    dve.wait_ge(mix_full, u.full)
                    o1 = mix_ps[:, u.bank, 0:H1 * (DH + 1)].rearrange("p (h d) -> p h d", h=H1)
                    nc.vector.reciprocal(inv_lsum[:, :], o1[:, :, DH]).then_inc(inv_lsum_done, 1)
                    dve.wait_ge(inv_lsum_done, s.at(lambda t: t - 4 + 1))
                    nc.vector.tensor_tensor(o1_sb[:, :].rearrange("p (h d) -> p h d", h=H1), o1[:, :, 0:DH],
                                            inv_lsum[:, :].unsqueeze(2).broadcast_to([P, H1, DH]),
                                            ALU.mult).then_inc(mix_out[u.bank], 1)
                if s.has(0):
                    dve.wait_ge(x1_done, s.at(lambda t: t + 1))
                    nc.vector.bn_stats(stats1[:, :], x1[:, s.n % 4, :]).then_inc(stats1_done, 1)
                    dve.wait_ge(stats1_done, s.at(lambda t: t + 1))
                    wait(dve, ln1_step, s.at(lambda t: 4 * t))
                    settle(dve, settled_dve, s.i)
                    nc.vector.bn_aggr(mv1[:, :], stats1[:, :]).then_inc(mv1_done, 1)
                if not s.odd and s.has(2):
                    v_rows(s, "va", 2)
                if s.odd and s.has(-3):
                    for c in range(C1):
                        u = s.proj(f"lq{c}")
                        if c == 1:
                            if s.has(3):
                                lo_part(s, "ht0", h_t[1][:, :, 0:P], h_t[0][:, :, 0:P])
                            if s.has(-4):
                                lo_part(s, "o1t", o_t[1][:, :, :], o_t[0][:, :, :])
                        dve.wait_ge(proj_full, u.full)
                        nc.vector.tensor_copy(lq_t[:, c, :], proj_ps[:, u.bank, 0:2 * P]).then_inc(proj_out[u.bank], 1)
                else:
                    if s.odd and s.has(3):
                        lo_part(s, "ht0", h_t[1][:, :, 0:P], h_t[0][:, :, 0:P])
                    if s.has(-4):
                        lo_part(s, "o1t", o_t[1][:, :, :], o_t[0][:, :, :])
                if s.odd and s.has(4):
                    lo_part(s, "ht1", h_t[1][:, :, P:2 * P], h_t[0][:, :, P:2 * P])
                if s.odd and s.has(-3):
                    copy_bd(s, "lk0", lk_bd, 0, None)
                if s.odd and s.has(1):
                    directions(s, 0)
                if s.odd and s.has(-1):
                    lo_part(s, "h1t0", h1_t[1][:, :, 0:P], h1_t[0][:, :, 0:P])
                if s.odd and s.has(1):
                    direction_blocks(s, 0)
                    directions(s, 1)
                if not s.odd and s.has(3):
                    v_rows(s, "vb", 3)
                if s.has(-4):
                    u = s.proj("wo")
                    dve.wait_ge(proj_full, u.full)
                    dve.wait_ge(y_base, s.at(lambda t: t - 4 + 1))
                    nc.vector.tensor_tensor(ybuf[:, :], proj_ps[:, u.bank, :], ybuf[:, :],
                                            ALU.add).then_inc(proj_out[u.bank], 1)
                if s.odd and s.has(1):
                    direction_blocks(s, 1)
                if s.odd and s.has(0):
                    lo_part(s, "h1t1", h1_t[1][:, :, P:2 * P], h1_t[0][:, :, P:2 * P])

            over_slots(dve, B, slot)

        @block.tensor
        def _(pe):
            def three_passes(ps, w, w_part, mv, mv_part):
                passes = [(c, a, b) for c in range(w[0].shape[1]) for a, b in ((0, 0), (0, 1), (1, 0))]
                for n, (c, a, b) in enumerate(passes):
                    ins = nc.tensor.matmul(ps, w[a][:, c, w_part], mv[b][:, c, mv_part],
                                           start=n == 0, stop=n == len(passes) - 1)
                return ins

            pe.wait_ge(w_in, 16 * W_LOADS)
            pe.wait_ge(consts, 7)
            everything = slice(0, D)
            for u, (kind, dst, part) in enumerate(PREP):
                ps = prep_bank(u)
                needs = u if kind in ("bias",) or (kind == "split" and dst is not w_m) and part == 0 else u - 3
                wait(pe, prep_copied, needs)
                cols = slice(part * P, (part + 1) * P) if isinstance(part, int) else None
                if kind == "split" and dst is w_m:
                    for c in range(C):
                        ins = nc.tensor.transpose(ps[:, c * P:(c + 1) * P], st_map[:, c, cols], ident[:, :])
                elif kind == "turn":
                    for c in range(C):
                        ins = nc.tensor.transpose(ps[:, c * P:(c + 1) * P], dst[:, c, cols], ident[:, :])
                elif kind == "split" and dst is w_v:
                    for c in range(C):
                        ins = nc.tensor.matmul(ps[:, c * P:(c + 1) * P], st_gcn[:, c, cols], gcn_bd_t[:, :],
                                               start=True, stop=True)
                elif kind == "split":
                    for c in range(C):
                        ins = nc.tensor.matmul(ps, st_map[:, c, cols], st_t[:, c, everything],
                                               start=c == 0, stop=c == C - 1)
                elif kind == "bias":
                    for o in range(C):
                        for c in range(C):
                            ins = nc.tensor.matmul(ps[:, o:o + 1], st_t[:, c, o * P:(o + 1) * P],
                                                   col_map_b[:, c:c + 1], start=c == 0, stop=c == C - 1)
                elif kind == "gcn":
                    ins = nc.tensor.transpose(ps[:, 0:P], gcn_bd[:, :], ident[:, :])
                else:
                    for c in range(C):
                        ins = nc.tensor.matmul(ps[:, c * P:(c + 1) * P], col_gb[:, c:c + 1].broadcast_to([P, P]),
                                               gcn_bd_t[:, :], start=True, stop=True)
                ins.then_inc(prep_full, 1)
            pe.wait_ge(prep_copied, len(PREP))
            pe.wait_ge(lw_done, 4)
            pe.wait_ge(ones_in, 5)

            def start_proj(s, name):
                u = s.proj(name)
                wait(pe, proj_out[u.bank], u.before)
                return proj_ps[:, u.bank]

            def start_mix(s, name):
                u = s.mix(name)
                wait(pe, mix_out[u.bank], u.before)
                return mix_ps[:, u.bank]

            both = slice(0, 2 * P)

            def features(s, name, w, c, h):
                ps = start_proj(s, name)
                three_passes(ps[:, 0:2 * P], w, slice(c * P, (c + 1) * P), h, both).then_inc(proj_full, 1)

            def rows(s, name, w, width, h, g):
                ps = start_proj(s, name)
                three_passes(ps[:, 0:width], h, slice(g * P, (g + 1) * P), w, slice(0, width)).then_inc(proj_full, 1)

            def turn(s, name, src):
                ps = start_mix(s, name)
                for c in range(C):
                    ins = nc.tensor.transpose(ps[:, c * P:(c + 1) * P], src[:, c * P:(c + 1) * P], ident[:, :])
                ins.then_inc(mix_full, 1)

            def spread_inv_norm(s, g):
                pe.wait_ge(inv_rows_done, s.at(lambda t: t + 2 + g))
                ps = start_mix(s, f"bc{g}")
                for c in range(C):
                    ins = nc.tensor.transpose(ps[:, c * P:(c + 1) * P],
                                              p1_t[:, c, :], ident[:, :])
                ins.then_inc(mix_full, 1)

            def l1_scores(s):
                if not s.odd:
                    for c in range(2):
                        u = s.proj(f"lk{c}", back=1)
                        pe.wait_ge(proj_out[u.bank], u.before + 1)
                g = s.n % 2
                ps = start_mix(s, "s1")
                for c in range(C1):
                    ins = nc.tensor.matmul(ps[:, c * 2 * P:(c + 1) * 2 * P], lq_t[:, c, g * P:(g + 1) * P],
                                           lk_bd[:, c, g, :, :], start=True, stop=True)
                ins.then_inc(mix_full, 1)

            def scores(s):
                if not s.odd:
                    for c in (2, 3):
                        u = s.proj(f"k{c}", back=1)
                        pe.wait_ge(proj_out[u.bank], u.before + 1)
                wait(pe, ect_act, s.at(lambda t: t))
                wait(pe, ect_dve, s.at(lambda t: t))
                g = s.n % 2
                for c in range(C):
                    ins = nc.tensor.matmul(s_ps[:, c // 2, c % 2 * 2:c % 2 * 2 + 2, :], q_t[:, c, g * P:(g + 1) * P],
                                           k_bd[:, c, g, :, :], start=True, stop=True)
                ins.then_inc(s_full, 1)

            def cosines(s):
                pe.wait_ge(dir_done, s.at(lambda t: t + 1))
                wait(pe, av_scaled, s.at(lambda t: t))
                g = s.n % 2
                for c in range(C):
                    for n, (a, b) in enumerate(((0, 0), (0, 1), (1, 0))):
                        ins = nc.tensor.matmul(c_ps[:, c // 2, c % 2 * 2 * P:(c % 2 + 1) * 2 * P],
                                               dir_t[:, a, c, g * P:(g + 1) * P], dir_bd[:, b, c, g, :],
                                               start=n == 0, stop=n == 2)
                ins.then_inc(c_full, 1)

            def turn_e(s):
                pe.wait_ge(ec_done, s.at(lambda t: t + 1))
                for h in range(H):
                    ins = nc.tensor.transpose(s_ps[:, h // 4, h % 4, :], e_sb[:, h, :], ident[:, :])
                ins.then_inc(ect_full, 1)

            def weighted_sums(s):
                pe.wait_ge(ect_act, s.at(lambda t: t + 1))
                pe.wait_ge(ect_dve, s.at(lambda t: t + 1))
                for h in range(H):
                    ins = nc.tensor.matmul(av(h // 4)[:, h % 4, :], ec_t[:, h, :], v_sb[:, s.n % 4, h, :],
                                           start=True, stop=True)
                ins.then_inc(av_full, 1)

            def turn_p1(s):
                pe.wait_ge(p1_done, s.at(lambda t: t - 4 + 1))
                ps = start_mix(s, "p1t")
                for h in range(H1):
                    ins = nc.tensor.transpose(ps[:, h * P:(h + 1) * P], p1_sb[:, h, :], ident[:, :])
                ins.then_inc(mix_full, 1)

            def l1_sums(s):
                u = s.mix("p1t")
                pe.wait_ge(mix_out[u.bank], u.before + 1)
                ps = start_mix(s, "o1")
                for h in range(H1):
                    ins = nc.tensor.matmul(ps[:, h * (DH + 1):(h + 1) * (DH + 1)], p1_t[:, h, :],
                                           lv_sb[:, s.n % 4, h, :], start=True, stop=True)
                ins.then_inc(mix_full, 1)

            def turn_o1(s):
                u = s.mix("o1")
                pe.wait_ge(mix_out[u.bank], u.before + 1)
                ps = start_mix(s, "o1t")
                for c in range(C1):
                    ins = nc.tensor.transpose(ps[:, c * P:(c + 1) * P], o1_sb[:, c * P:(c + 1) * P], ident[:, :])
                ins.then_inc(mix_full, 1)

            def output(s):
                u = s.mix("o1t")
                pe.wait_ge(mix_out[u.bank], u.before + 1)
                ps = start_proj(s, "wo")
                three_passes(ps, o_t, slice(0, P), w_o, everything).then_inc(proj_full, 1)

            def slot(s):
                if s.has(-4):
                    l1_scores(s)
                if s.has(0):
                    scores(s)
                    cosines(s)
                if s.odd:
                    if s.has(1):
                        features(s, "q0", w_q, 0, h_t)
                        features(s, "q1", w_q, 1, h_t)
                        features(s, "q2", w_q, 2, h_t)
                        features(s, "q3", w_q, 3, h_t)
                        pe.wait_ge(squared, s.at(lambda t: (t + 1) // 2 + 1))
                        ps = start_mix(s, "norm")
                        for g in range(2):
                            for c in range(C):
                                ins = nc.tensor.matmul(ps[:, g * H:(g + 1) * H], sq_t[:, c, g * P:(g + 1) * P],
                                                       head_sel[:, c, :], start=c == 0, stop=c == C - 1)
                        ins.then_inc(mix_full, 1)
                    if s.has(0):
                        turn_e(s)
                    if s.has(1):
                        features(s, "k0", w_k, 0, h_t)
                        features(s, "k1", w_k, 1, h_t)
                    if s.has(-4):
                        turn_p1(s)
                    if s.has(0):
                        weighted_sums(s)
                    if s.has(1):
                        features(s, "k2", w_k, 2, h_t)
                        features(s, "k3", w_k, 3, h_t)
                    if s.has(-4):
                        l1_sums(s)
                    if s.has(-3):
                        features(s, "lq0", w_lq, 0, h1_t)
                    if s.has(3):
                        pe.wait_ge(h_done, s.at(lambda t: t + 5))
                        turn(s, "ht0", xa[:, 0, :])
                    if s.has(-4):
                        turn_o1(s)
                    if s.has(-3):
                        features(s, "lq1", w_lq, 1, h1_t)
                    if s.has(4):
                        turn(s, "ht1", xa[:, 1, :])
                    if s.has(-3):
                        features(s, "lk0", w_lk, 0, h1_t)
                    if s.has(1):
                        spread_inv_norm(s, 0)
                    if s.has(-3):
                        features(s, "lk1", w_lk, 1, h1_t)
                    if s.has(-1):
                        pe.wait_ge(h1_done, s.at(lambda t: t))
                        turn(s, "h1t0", h1_sb[:, 0, :])
                    if s.has(2):
                        spread_inv_norm(s, 1)
                    if s.has(-4):
                        output(s)
                    if s.has(0):
                        pe.wait_ge(h1_done, s.at(lambda t: t + 1))
                        turn(s, "h1t1", h1_sb[:, 1, :])
                else:
                    if s.has(2):
                        u = s.mix("ht1", back=1)
                        pe.wait_ge(mix_out[u.bank], u.before + 1)
                        for c in range(C):
                            features(s, f"m{c}", w_m, c, h_t)
                    if s.has(0):
                        turn_e(s)
                    if s.has(-2):
                        u = s.mix("h1t1", back=1)
                        pe.wait_ge(mix_out[u.bank], u.before + 1)
                        rows(s, "v1a", w_lv, INNER, h1_t, 0)
                        rows(s, "v1b", w_lv, INNER, h1_t, 1)
                    if s.has(-4):
                        turn_p1(s)
                    if s.has(0):
                        weighted_sums(s)
                    if s.has(2):
                        rows(s, "va", w_v, D, h_t, 0)
                    if s.has(-4):
                        l1_sums(s)
                    if s.has(2):
                        rows(s, "vb", w_v, D, h_t, 1)
                    if s.has(-4):
                        turn_o1(s)
                    if s.has(-4):
                        output(s)

            over_slots(pe, B, slot)


def kernel(**inputs):
    import numpy as np
    import concourse.bacc as bacc
    from concourse.bass_utils import run_bass_kernel_spmd

    names = ["x", "adj", "L0_gnn_map_w", "L0_gnn_map_b", "L0_gnn_q_w", "L0_gnn_q_b", "L0_gnn_k_w", "L0_gnn_k_b",
             "L0_gnn_gcn_map_w", "L0_gnn_gcn_map_b", "L0_gnn_gcn_W", "L1_gnn_Wq", "L1_gnn_Wk", "L1_gnn_Wv",
             "L1_gnn_Wo", "L1_gnn_bo"]
    nc = bacc.Bacc("TRN2", target_bir_lowering=False, num_devices=1)
    arrays, args = {}, []
    for name in names:
        a = np.ascontiguousarray(inputs[name])
        arrays[f"in_{name}_dram"] = a
        args.append(nc.dram_tensor(f"in_{name}_dram", a.shape, mybir.dt.from_np(a.dtype), kind="ExternalInput").ap())
    shape = arrays["in_x_dram"].shape
    args.append(nc.dram_tensor("out_dram", shape, F32, kind="ExternalOutput").ap())
    build(nc, *args)
    return run_bass_kernel_spmd(nc, [arrays], core_ids=[0]).results[0]["out_dram"]
```
